# Optimizing a Trainium2 kernel written in Bass

```python
import numpy as np
import jax
import jax.numpy as jnp

def _softmax(x, axis=-1):
    return jax.nn.softmax(x, axis=axis)

def _gelu(x):
    return jax.nn.gelu(x, approximate=True)

def _silu(x):
    return jax.nn.silu(x)

def _sigmoid(x):
    return jax.nn.sigmoid(x)

def _layernorm(x, axis=-1, eps=1e-05):
    m = jnp.mean(x, axis=axis, keepdims=True)
    v = jnp.var(x, axis=axis, keepdims=True)
    return (x - m) / jnp.sqrt(v + eps)

def _scatter_add(tgt, idx, src, axis=0):
    return tgt.at[idx].add(src)

def _segment_sum(src, seg, n):
    return jax.ops.segment_sum(src, seg, n)
kernel_name = 'mk_gnn_preln_d4_gnn_r8_7a4ad5'

def setup_inputs(seed: int=0):
    np.random.seed(seed)
    _w = jnp.asarray

    def _rec_inputs():
        import jax
        import jax.numpy as jnp
        _gk = jax.random.key(seed)
        x = -0.0002928 + 1 * jax.random.normal(jax.random.fold_in(_gk, 1), (6250, 64), jnp.float32)
        _s = jax.random.randint(jax.random.fold_in(_gk, 2), (100000,), 0, 6250, jnp.int32)
        _d = jax.random.randint(jax.random.fold_in(_gk, 3), (100000,), 0, 6250, jnp.int32)
        _loop = jnp.arange(6250, dtype=jnp.int32)
        src = jnp.concatenate([_s, _d, _loop])
        dst = jnp.concatenate([_d, _s, _loop])
        _o = jnp.argsort(dst, stable=True)
        src = src[_o]
        dst = dst[_o]
        edge_attr_16 = 0.000216709 + 1.00012 * jax.random.normal(jax.random.fold_in(_gk, 12), (206250, 16), jnp.float32)
        edge_attr_64 = -9.77346e-05 + 0.999888 * jax.random.normal(jax.random.fold_in(_gk, 13), (206250, 64), jnp.float32)
        edge_weight = jax.random.uniform(jax.random.fold_in(_gk, 15), (206250,), jnp.float32, 0.0, 0.999999)
        edge_weight_n2 = jax.random.uniform(jax.random.fold_in(_gk, 16), (206250,), jnp.float32, 0.0, 0.999999)
        return (x, src, dst, edge_attr_16, edge_attr_64, edge_weight, edge_weight_n2)
    x, src, dst, edge_attr_16, edge_attr_64, edge_weight, edge_weight_n2 = _rec_inputs()

    def _L0_gnn_setup():
        import jax, jax.numpy as jnp
        import numpy as np
        N, E, D_IN, D_OUT = (8192, 131072, 64, 64)
        EPS = 1e-08
        key = jax.random.key(seed)
        ks = jax.random.split(key, 8)
        h = jax.random.normal(ks[0], (N, D_IN), dtype=jnp.float32)
        edge_index = jax.random.randint(ks[1], (2, E), 0, N, dtype=jnp.int64 if jax.config.jax_enable_x64 else jnp.int32)
        adj_v = jax.random.uniform(ks[2], (E,), dtype=jnp.float32)
        deg_v = jax.random.uniform(ks[3], (E,), dtype=jnp.float32)
        W = jax.random.normal(ks[4], (D_IN, D_OUT), dtype=jnp.float32) / np.sqrt(D_IN)
        b = jax.random.normal(ks[5], (D_OUT,), dtype=jnp.float32) * 0.01
        deg_coeff = jnp.array([0.5, 0.0], dtype=jnp.float32)
        coeff_param = jnp.zeros((3,), dtype=jnp.float32)
        scale_param = 2.0 * jnp.ones((1,), dtype=jnp.float32)
        return {'h': h, 'edge_index': edge_index, 'adj_v': adj_v, 'deg_v': deg_v, 'W': W, 'b': b, 'deg_coeff': deg_coeff, 'coeff_param': coeff_param, 'scale_param': scale_param}
    _L0_gnn_all = _L0_gnn_setup()
    _L0_gnn_in = {k: v for k, v in _L0_gnn_all.items() if k in ('W', 'b', 'deg_coeff', 'coeff_param', 'scale_param')}
    del _L0_gnn_all

    def _L1_gnn_setup():
        import jax, jax.numpy as jnp
        import numpy as np
        N_NODES = 6250
        N_EDGES = 100000
        H_DIM = 64

        def scatter_mean(e, receiver, num_segments):
            sums = jax.ops.segment_sum(e, receiver, num_segments=num_segments)
            counts = jax.ops.segment_sum(jnp.ones((e.shape[0],), e.dtype), receiver, num_segments=num_segments)
            return sums / jnp.maximum(counts, 1.0)[:, None]
        key = jax.random.key(seed)
        ks = jax.random.split(key, 10)
        h = H_DIM
        v = jax.random.normal(ks[0], (N_NODES, h), dtype=jnp.float32)
        e = jax.random.normal(ks[1], (N_EDGES, h), dtype=jnp.float32)
        edge_index = jax.random.randint(ks[2], (2, N_EDGES), 0, N_NODES, dtype=jnp.int64)

        def glorot(k, shape):
            fan_in, fan_out = shape
            lim = np.sqrt(6.0 / (fan_in + fan_out)).astype(np.float32)
            return jax.random.uniform(k, shape, jnp.float32, -lim, lim)
        W0 = glorot(ks[3], (2 * h, h))
        b0 = jnp.zeros((h,), jnp.float32)
        W1 = glorot(ks[4], (h, h))
        b1 = jnp.zeros((h,), jnp.float32)
        W2 = glorot(ks[5], (h, h))
        b2 = jnp.zeros((h,), jnp.float32)
        return {'v': v, 'edge_index': edge_index, 'e': e, 'W0': W0, 'b0': b0, 'W1': W1, 'b1': b1, 'W2': W2, 'b2': b2}
    _L1_gnn_all = _L1_gnn_setup()
    _L1_gnn_in = {k: v for k, v in _L1_gnn_all.items() if k in ('W0', 'b0', 'W1', 'b1', 'W2', 'b2')}
    del _L1_gnn_all

    def _L2_gnn_setup():
        import jax, jax.numpy as jnp
        import numpy as np
        N, C_IN, C_OUT, K = (12500, 64, 64, 16)
        E = N * K
        BN_EPS = 1e-05

        def _bn(h, gamma, beta):
            mean = jnp.mean(h, axis=0)
            var = jnp.mean(jnp.square(h - mean), axis=0)
            return (h - mean) * jax.lax.rsqrt(var + BN_EPS) * gamma + beta
        key = jax.random.key(seed)
        ks = jax.random.split(key, 4)
        x = jax.random.normal(ks[0], (N, C_IN), dtype=jnp.float32)
        edge_row = jnp.repeat(jnp.arange(N, dtype=jnp.int64), K)
        edge_col = jax.random.randint(ks[1], (E,), 0, N).astype(jnp.int64)
        W1 = jax.random.normal(ks[2], (2 * C_IN, C_OUT), dtype=jnp.float32) * (1.0 / np.sqrt(2 * C_IN))
        W2 = jax.random.normal(ks[3], (C_OUT, C_OUT), dtype=jnp.float32) * (1.0 / np.sqrt(C_OUT))
        return {'x': x, 'edge_row': edge_row, 'edge_col': edge_col, 'W1': W1, 'b1': jnp.zeros((C_OUT,), jnp.float32), 'g1': jnp.ones((C_OUT,), jnp.float32), 'be1': jnp.zeros((C_OUT,), jnp.float32), 'W2': W2, 'b2': jnp.zeros((C_OUT,), jnp.float32), 'g2': jnp.ones((C_OUT,), jnp.float32), 'be2': jnp.zeros((C_OUT,), jnp.float32)}
    _L2_gnn_all = _L2_gnn_setup()
    _L2_gnn_in = {k: v for k, v in _L2_gnn_all.items() if k in ('W1', 'b1', 'g1', 'be1', 'W2', 'b2', 'g2', 'be2')}
    del _L2_gnn_all

    def _L3_gnn_setup():
        import jax, jax.numpy as jnp
        import numpy as np
        N = 12500
        E = 200000
        F_IN = 64
        F_HID = 128
        F_EDGE = 16
        CUTOFF = 5.0
        IN_DIM = 2 * F_IN + F_EDGE + 1
        key = jax.random.key(seed)
        ks = jax.random.split(key, 12)

        def lin(k, fan_in, fan_out):
            bound = 1.0 / np.sqrt(fan_in)
            kw, kb = jax.random.split(k)
            W = jax.random.uniform(kw, (fan_in, fan_out), jnp.float32, -bound, bound)
            b = jax.random.uniform(kb, (fan_out,), jnp.float32, -bound, bound)
            return (W, b)
        x = jax.random.normal(ks[0], (N, F_IN), jnp.float32)
        edge_index = jax.random.randint(ks[1], (2, E), 0, N, jnp.int32)
        edge_weight = jax.random.uniform(ks[2], (E,), jnp.float32)
        edge_attr = jax.random.normal(ks[3], (E, F_EDGE), jnp.float32)
        ew1, eb1 = lin(ks[4], IN_DIM, F_HID)
        ew2, eb2 = lin(ks[5], F_HID, F_HID)
        nw1, nb1 = lin(ks[6], F_IN + F_HID, F_HID)
        nw2, nb2 = lin(ks[7], F_HID, F_IN)
        return {'x': x, 'edge_index': edge_index, 'edge_weight': edge_weight, 'edge_attr': edge_attr, 'ew1': ew1, 'eb1': eb1, 'ew2': ew2, 'eb2': eb2, 'nw1': nw1, 'nb1': nb1, 'nw2': nw2, 'nb2': nb2}
    _L3_gnn_all = _L3_gnn_setup()
    _L3_gnn_in = {k: v for k, v in _L3_gnn_all.items() if k in ('ew1', 'eb1', 'ew2', 'eb2', 'nw1', 'nb1', 'nw2', 'nb2')}
    del _L3_gnn_all
    return {'x': x, 'src': src, 'dst': dst, 'edge_attr_16': edge_attr_16, 'edge_attr_64': edge_attr_64, 'edge_weight': edge_weight, 'edge_weight_n2': edge_weight_n2, 'L0_gnn_W': _L0_gnn_in['W'], 'L0_gnn_b': _L0_gnn_in['b'], 'L0_gnn_deg_coeff': _L0_gnn_in['deg_coeff'], 'L0_gnn_coeff_param': _L0_gnn_in['coeff_param'], 'L0_gnn_scale_param': _L0_gnn_in['scale_param'], 'L1_gnn_W0': _L1_gnn_in['W0'], 'L1_gnn_b0': _L1_gnn_in['b0'], 'L1_gnn_W1': _L1_gnn_in['W1'], 'L1_gnn_b1': _L1_gnn_in['b1'], 'L1_gnn_W2': _L1_gnn_in['W2'], 'L1_gnn_b2': _L1_gnn_in['b2'], 'L2_gnn_W1': _L2_gnn_in['W1'], 'L2_gnn_b1': _L2_gnn_in['b1'], 'L2_gnn_g1': _L2_gnn_in['g1'], 'L2_gnn_be1': _L2_gnn_in['be1'], 'L2_gnn_W2': _L2_gnn_in['W2'], 'L2_gnn_b2': _L2_gnn_in['b2'], 'L2_gnn_g2': _L2_gnn_in['g2'], 'L2_gnn_be2': _L2_gnn_in['be2'], 'L3_gnn_ew1': _L3_gnn_in['ew1'], 'L3_gnn_eb1': _L3_gnn_in['eb1'], 'L3_gnn_ew2': _L3_gnn_in['ew2'], 'L3_gnn_eb2': _L3_gnn_in['eb2'], 'L3_gnn_nw1': _L3_gnn_in['nw1'], 'L3_gnn_nb1': _L3_gnn_in['nb1'], 'L3_gnn_nw2': _L3_gnn_in['nw2'], 'L3_gnn_nb2': _L3_gnn_in['nb2']}

def reference(x, src, dst, edge_attr_16, edge_attr_64, edge_weight, edge_weight_n2, L0_gnn_W, L0_gnn_b, L0_gnn_deg_coeff, L0_gnn_coeff_param, L0_gnn_scale_param, L1_gnn_W0, L1_gnn_b0, L1_gnn_W1, L1_gnn_b1, L1_gnn_W2, L1_gnn_b2, L2_gnn_W1, L2_gnn_b1, L2_gnn_g1, L2_gnn_be1, L2_gnn_W2, L2_gnn_b2, L2_gnn_g2, L2_gnn_be2, L3_gnn_ew1, L3_gnn_eb1, L3_gnn_ew2, L3_gnn_eb2, L3_gnn_nw1, L3_gnn_nb1, L3_gnn_nw2, L3_gnn_nb2):
    import jax
    import jax.numpy as jnp

    def _L0_gnn_ref(h, edge_index, adj_v, deg_v, W, b, deg_coeff, coeff_param, scale_param):
        import jax, jax.numpy as jnp
        import numpy as np
        N, E, D_IN, D_OUT = (8192, 131072, 64, 64)
        EPS = 1e-08
        n_nodes = h.shape[0]
        Wh = h @ W + b
        row, col = (edge_index[0], edge_index[1])
        sc = jax.nn.softplus(deg_coeff[0] * deg_v + deg_coeff[1])
        Wr = Wh[row]
        Wc = Wh[col]
        dot = jnp.sum(Wr * Wc, axis=-1)
        nr = jnp.sqrt(jnp.sum(Wr * Wr, axis=-1))
        nc = jnp.sqrt(jnp.sum(Wc * Wc, axis=-1))
        sim = dot / jnp.maximum(nr * nc, EPS)
        sim_pos = jax.nn.relu(sim)
        sim_neg = -jax.nn.relu(-sim)
        no_diag = (row != col).astype(Wh.dtype)
        base = adj_v * sc * no_diag
        prop_pos = jax.ops.segment_sum((base * sim_pos)[:, None] * Wc, row, num_segments=n_nodes)
        prop_neg = jax.ops.segment_sum((base * sim_neg)[:, None] * Wc, row, num_segments=n_nodes)
        coeff = jax.nn.softmax(coeff_param)
        scale = jax.nn.softplus(scale_param)
        return scale * (coeff[0] * prop_pos + coeff[1] * prop_neg + coeff[2] * Wh)

    def _L1_gnn_ref(v, edge_index, e, W0, b0, W1, b1, W2, b2):
        import jax, jax.numpy as jnp
        import numpy as np
        N_NODES = 6250
        N_EDGES = 100000
        H_DIM = 64

        def scatter_mean(e, receiver, num_segments):
            sums = jax.ops.segment_sum(e, receiver, num_segments=num_segments)
            counts = jax.ops.segment_sum(jnp.ones((e.shape[0],), e.dtype), receiver, num_segments=num_segments)
            return sums / jnp.maximum(counts, 1.0)[:, None]
        receiver = edge_index[1]
        agg = scatter_mean(e, receiver, v.shape[0])
        x = jnp.concatenate([agg, v], axis=-1)
        x = jax.nn.relu(x @ W0 + b0)
        x = jax.nn.relu(x @ W1 + b1)
        x = x @ W2 + b2
        return x

    def _L2_gnn_ref(x, edge_row, edge_col, W1, b1, g1, be1, W2, b2, g2, be2):
        import jax, jax.numpy as jnp
        import numpy as np
        N, C_IN, C_OUT, K = (12500, 64, 64, 16)
        E = N * K
        BN_EPS = 1e-05

        def _bn(h, gamma, beta):
            mean = jnp.mean(h, axis=0)
            var = jnp.mean(jnp.square(h - mean), axis=0)
            return (h - mean) * jax.lax.rsqrt(var + BN_EPS) * gamma + beta
        xi = x[edge_row]
        xj = x[edge_col]
        feat = jnp.concatenate([xi, xj - xi], axis=1)
        h = jax.nn.relu(_bn(feat @ W1 + b1, g1, be1))
        h = jax.nn.relu(_bn(h @ W2 + b2, g2, be2))
        out = jax.ops.segment_max(h, edge_row, num_segments=x.shape[0])
        return out

    def _L3_gnn_ref(x, edge_index, edge_weight, edge_attr, ew1, eb1, ew2, eb2, nw1, nb1, nw2, nb2):
        import jax, jax.numpy as jnp
        import numpy as np
        N = 12500
        E = 200000
        F_IN = 64
        F_HID = 128
        F_EDGE = 16
        CUTOFF = 5.0
        IN_DIM = 2 * F_IN + F_EDGE + 1
        row, col = (edge_index[0], edge_index[1])
        d_raw = (edge_weight / CUTOFF)[:, None]
        edge_input = jnp.concatenate([x[row], x[col], edge_attr, d_raw], axis=-1)
        h = jax.nn.silu(edge_input @ ew1 + eb1)
        m_ij = jax.nn.silu(h @ ew2 + eb2)
        agg = jax.ops.segment_sum(m_ij, row, num_segments=x.shape[0])
        node_in = jnp.concatenate([x, agg], axis=-1)
        upd = jax.nn.silu(node_in @ nw1 + nb1) @ nw2 + nb2
        return x + upd
    edge_index = jnp.stack([src, dst])
    h = jnp.maximum(_layernorm(x, axis=-1), 0.0)
    x = x + _L0_gnn_ref(h, edge_index, edge_weight, edge_weight_n2, L0_gnn_W, L0_gnn_b, L0_gnn_deg_coeff, L0_gnn_coeff_param, L0_gnn_scale_param)
    h = jnp.maximum(_layernorm(x, axis=-1), 0.0)
    x = x + _L1_gnn_ref(h, edge_index, edge_attr_64, L1_gnn_W0, L1_gnn_b0, L1_gnn_W1, L1_gnn_b1, L1_gnn_W2, L1_gnn_b2)
    h = jnp.maximum(_layernorm(x, axis=-1), 0.0)
    x = x + _L2_gnn_ref(h, src, dst, L2_gnn_W1, L2_gnn_b1, L2_gnn_g1, L2_gnn_be1, L2_gnn_W2, L2_gnn_b2, L2_gnn_g2, L2_gnn_be2)
    h = jnp.maximum(_layernorm(x, axis=-1), 0.0)
    x = x + _L3_gnn_ref(h, edge_index, edge_weight, edge_attr_16, L3_gnn_ew1, L3_gnn_eb1, L3_gnn_ew2, L3_gnn_eb2, L3_gnn_nw1, L3_gnn_nb1, L3_gnn_nw2, L3_gnn_nb2)
    return x

_drawn_inputs = setup_inputs


def setup_inputs(seed=0):
    import zlib

    import numpy as np

    out = dict(_drawn_inputs(seed))
    spreads = {'L0_gnn_coeff_param': (0.0, 0.1),
     'L1_gnn_b0': (0.0, 0.301),
     'L1_gnn_b1': (0.0, 0.275),
     'L1_gnn_b2': (0.0, 0.1),
     'L2_gnn_b1': (0.0, 2.0),
     'L2_gnn_g1': (1.0, 0.2),
     'L2_gnn_be1': (0.0, 0.277),
     'L2_gnn_b2': (0.0, 2.0),
     'L2_gnn_g2': (1.0, 0.2),
     'L2_gnn_be2': (0.0, 0.1)}
    factors = {'edge_attr_16': 6.406,
     'L0_gnn_b': 2.776,
     'L3_gnn_eb1': 4.684,
     'L3_gnn_nb1': 8.0,
     'L3_gnn_nb2': 3.612}
    for name, (base, spread) in spreads.items():
        noise = np.random.default_rng([zlib.crc32(name.encode()), seed]).standard_normal(out[name].shape)
        drawn = base * np.exp(spread * noise) if base else spread * noise
        out[name] = jnp.asarray(drawn.astype(out[name].dtype))
    for name, factor in factors.items():
        out[name] = (out[name] * factor).astype(out[name].dtype)
    return out
```

```python
from contextlib import ExitStack, contextmanager

import concourse.bass as bass
from concourse import mybir

ALU = mybir.AluOpType
ACT = mybir.ActivationFunctionType
AX_X = mybir.AxisListType.X
F32 = mybir.dt.float32
BF16 = mybir.dt.bfloat16
I32 = mybir.dt.int32

P = 128
D = 64
HID = 128
DE = 16
N = 6250
E = 206250
T = 4
UE = T * P
UNITS = 404
HU = UNITS // 2
EP = UNITS * UE
HALF = HU * UE
LO = 64
NJ = 52
NP = P * NJ
HI = NP // LO
NB = NJ // 4
TABLES = 8
RW = 20
FULL = E // UE
REST = E - FULL * UE
RESTP, RESTK = REST // T, REST % T
LN_EPS = 1e-5
BN_EPS = 1e-5
COS_EPS = 1e-8
BIG = 1e30


class Steps:

    def __init__(self, eng, sem, base=0):
        self.eng, self.sem, self.base, self.n = eng, sem, base, 0

    def done(self, ins):
        ins.then_inc(self.sem, 1)
        self.n += 1

    def wait(self):
        self.eng.wait_ge(self.sem, self.base + self.n)

    def run(self, ins):
        self.done(ins)
        self.wait()


def waited(eng, sem):
    eng.sem_inc(sem, 1)


def spread(ap, n):
    s = list(ap.shape)
    return ap.unsqueeze(len(s)).to_broadcast(s + [n])


def spread_mid(ap, n):
    s = list(ap.shape)
    return ap.unsqueeze(1).to_broadcast([s[0], n] + s[1:])


def start_at_one(c, sems):
    with c.nc.Block() as block:
        @block.gpsimd
        def _(pool):
            for sem in sems:
                pool.sem_inc(sem, 1)


def from_zero(eng, body, n):
    body(0)
    with eng.Fori(1, n) as i:
        body(i)


def used(i):
    return not (isinstance(i, int) and i == 0)


@contextmanager
def own_semaphores(c):
    nc, outer, mine = c.nc, c.sem, []

    def take(name):
        mine.append(nc.alloc_semaphore(name=name))
        return mine[-1]

    c.sem = take
    yield
    c.sem = outer
    with nc.Block() as block:
        @block.gpsimd
        def _(pool):
            for sem in mine:
                pool.sem_clear(sem)
    for sem in mine:
        nc.release_semaphore(sem)


class Core:
    pass


def make_constants(c, stack):
    nc = c.nc

    def sb(name, shape, dt=F32):
        return stack.enter_context(nc.sbuf_tensor(name, shape, dt))

    c.ident = sb("ident", [P, P])
    c.identb = sb("identb", [P, P], BF16)
    c.below = sb("below", [P, P])
    c.above = sb("above", [P, P])
    c.pairs = sb("pairs", [P, P])
    c.count_lo = sb("count_lo", [P, LO], BF16)
    c.count_hi = sb("count_hi", [P, HI], BF16)
    c.part_hi = sb("part_hi", [P, 1])
    c.spare_row = sb("spare_row", [P, T])
    c.spare_pos = sb("spare_pos", [P, NJ])
    c.ones = sb("ones", [P, LO])
    c.xs = sb("xs", [P, NJ, D])
    c.cnt = sb("cnt", [P, NJ])
    c.off = sb("off", [P, NJ])
    c.has = sb("has", [P, NJ])
    c.keep = sb("keep", [P, NJ])
    c.cross = sb("cross", [P, NJ])
    c.middle = sb("middle", [P, NJ])
    c.first = sb("first", [P, NJ], I32)
    c.last = sb("last", [P, NJ], I32)
    ramp = sb("ramp", [P, P], I32)
    ramp_p = sb("ramp_p", [P, 1], I32)
    ramp_n = sb("ramp_n", [P, NJ], I32)
    made, step, filled, x_in = (c.sem(n) for n in ("const_made", "const_step", "tables_filled", "x_loaded"))
    with ExitStack() as local, nc.Block() as block:
        zeros = local.enter_context(nc.sbuf_tensor("zeros", [P, 3445], F32))
        units = local.enter_context(nc.sbuf_tensor("units", [P, 1616], F32))

        @block.gpsimd
        def _(pool):
            st = Steps(pool, made)
            st.done(pool.memset(c.ident[:, :], 0.0))
            st.done(pool.memset(c.below[:, :], 1.0))
            st.done(pool.memset(c.above[:, :], 1.0))
            st.done(pool.iota(ramp[:, :], [[1, P]], 0, 0))
            st.done(pool.iota(ramp_p[:, :], [[0, 1]], 0, 1))
            st.done(pool.iota(ramp_n[:, :], [[1, NJ]], EP, NJ))
            st.wait()
            st.done(pool.affine_select(out=c.ident[:, :], in_=c.ident[:, :], compare_op=ALU.not_equal, fill=1.0,
                                       base=0, pattern=[[-1, P]], channel_multiplier=1))
            st.done(pool.affine_select(out=c.below[:, :], in_=c.below[:, :], compare_op=ALU.is_gt, fill=0.0,
                                       base=0, pattern=[[-1, P]], channel_multiplier=1))
            st.done(pool.affine_select(out=c.above[:, :], in_=c.above[:, :], compare_op=ALU.is_gt, fill=0.0,
                                       base=0, pattern=[[1, P]], channel_multiplier=-1))

        @block.vector
        def _(dve):
            st = Steps(dve, step)
            st.done(nc.vector.memset(zeros[:, :], 0.0))
            st.done(nc.vector.memset(units[:, :], 1.0))
            st.done(nc.vector.memset(c.xs[:, :, :], 0.0))
            nc.vector.memset(c.ones[:, :], 1.0)
            nc.vector.memset(c.pairs[:, :], 0.0)
            dve.wait_ge(made, 9)
            st.run(nc.vector.tensor_copy(c.identb[:, :], c.ident[:, :]))
            nc.vector.memset(c.pairs[0:64, 0:64], 1.0)
            nc.vector.memset(c.pairs[64:128, 64:128], 1.0)
            nc.vector.tensor_copy(c.count_lo[:, :], ramp[:, 0:LO])
            nc.vector.tensor_scalar(c.count_hi[:, :], ramp[:, 0:HI], float(LO), None, ALU.mult)
            nc.vector.tensor_scalar(c.part_hi[:, :], ramp_p[:, :], float(LO), None, ALU.mult)
            nc.vector.tensor_scalar(c.spare_row[:, :], ramp_p[:, 0:1].to_broadcast([P, T]), float(NP), None, ALU.add)
            nc.vector.tensor_copy(c.spare_pos[:, :], ramp_n[:, :])

        @block.sync
        def _(sp):
            full = N // NJ
            sp.wait_ge(step, 3)
            sp.dma_start(c.xs[0:full], c.x[0:full * NJ, :].rearrange("(p j) d -> p j d", p=full)).then_inc(x_in, 16)
            sp.dma_start(c.xs[full:full + 1, 0:N - full * NJ, :],
                         c.x[full * NJ:N, :].rearrange("(p j) d -> p j d", p=1)).then_inc(x_in, 16)
            for t in range(TABLES):
                sp.dma_start(c.agg_parts[t].rearrange("(p r) d -> p (r d)", p=P), zeros[:, :]).then_inc(filled, 16)
            sp.dma_start(c.same[0:EP, :].rearrange("(p r) o -> p (r o)", p=P), units[:, :]).then_inc(filled, 16)
            sp.wait_ge(filled, 16 * (TABLES + 1))
            sp.wait_ge(x_in, 32)


def lay_edges(c, KF, KB):
    nc = c.nc
    C, CU = 4, UNITS // 4
    loaded, padded, numbers, turned, taken, step, acts = (
        c.sem(n) for n in ("edges_loaded", "edges_padded", "edges_float", "edges_turned", "edges_taken",
                           "edges_step", "edges_act"))
    kf = KF[:, :].rearrange("p (u k f) -> p u k f", k=T, f=4)
    kb = KB[:, :].rearrange("p (u f k) -> p u f k", k=T, f=4)
    with ExitStack() as local:
        def sb(name, shape, dt=F32):
            return local.enter_context(nc.sbuf_tensor(name, shape, dt))

        raw_i = [sb(f"raw_i{a}", [CU, C, UE], I32) for a in range(2)]
        raw = [sb(f"raw{a}", [CU, C, UE]) for a in range(4)]
        deg = sb("deg", [P, UNITS, T])
        z, a, b = (sb(n, [P, UNITS, T]) for n in ("lay_z", "lay_a", "lay_b"))
        ti = sb("lay_i", [P, UNITS, T], I32)
        dc = sb("dc", [P, 2])
        turn = [local.enter_context(nc.psum_tensor(f"turn{s}", [P, 512], F32)) for s in range(2)]
        block = local.enter_context(nc.Block())
        sources = [c.src, c.dst, c.edge_weight, c.edge_weight_n2]
        places = raw_i + raw[2:]

        @block.sync
        def _(sp):
            sp.dma_start(dc[:, :], c.deg_coeff.partition_broadcast(P)).then_inc(loaded, 16)
            sp.wait_ge(padded, 1)
            last = FULL - 3 * CU
            for source, place in zip(sources, places):
                sp.dma_start(place[:, 0:3, :], source[0:3 * CU * UE].rearrange("(c u e) -> u c e", c=3, u=CU))\
                    .then_inc(loaded, 16)
                sp.dma_start(place[0:last, 3, :],
                             source[3 * CU * UE:FULL * UE].rearrange("(u e) -> u e", u=last)).then_inc(loaded, 16)
                sp.dma_start(place[last:last + 1, 3, 0:REST],
                             source[FULL * UE:E].rearrange("(u e) -> u e", u=1)).then_inc(loaded, 16)

        @block.tensor
        def _(pe):
            pe.wait_ge(numbers, 1)
            for n in range(4 * C):
                if n >= 2:
                    pe.wait_ge(taken, n - 1)
                for k in range(T):
                    src = raw[n // C][:, n % C, :].rearrange("u (e k) -> u k e", k=T)[:, k, :]
                    mm = nc.tensor.transpose(turn[n % 2][:, k * CU:(k + 1) * CU], src, c.ident[0:CU, 0:CU])
                mm.then_inc(turned, 1)

        @block.scalar
        def _(act):
            act.wait_ge(step, 1)
            nc.scalar.activation(a[:, :, :], z[:, :, :], ACT.Abs).then_inc(acts, 1)
            act.wait_ge(acts, 1)
            nc.scalar.activation(b[:, :, :], a[:, :, :], ACT.Exp, scale=-1.0).then_inc(acts, 1)
            act.wait_ge(acts, 2)
            nc.scalar.activation(a[:, :, :], b[:, :, :], ACT.Ln, bias=c.ones[:, 0:1]).then_inc(acts, 1)

        @block.vector
        def _(dve):
            v = nc.vector
            st = Steps(dve, step)
            for place, pad in zip(places, (N, N, 0, 0)):
                last = v.memset(place[:, 3, :], pad)
            last.then_inc(padded, 1)
            dve.wait_ge(loaded, 16 * 13)
            v.tensor_copy(raw[0][:, :, :], raw_i[0][:, :, :])
            v.tensor_copy(raw[1][:, :, :], raw_i[1][:, :, :]).then_inc(numbers, 1)
            into = [kf[:, :, :, 0], kf[:, :, :, 3], kf[:, :, :, 1], deg[:, :, :]]
            for n in range(4 * C):
                dve.wait_ge(turned, n + 1)
                u = (n % C) * CU
                v.tensor_copy(into[n // C][:, u:u + CU, :],
                              turn[n % 2][:, 0:T * CU].rearrange("p (k u) -> p u k", k=T)).then_inc(taken, 1)
            dve.wait_ge(taken, 4 * C)
            st.run(v.tensor_scalar(z[:, :, :], deg[:, :, :], dc[:, 0:1], dc[:, 1:2], ALU.mult, ALU.add))
            for f, node in ((0, kf[:, :, :, 0]), (2, kf[:, :, :, 3])):
                st.run(v.tensor_copy(ti[:, :, :], node))
                st.run(v.tensor_scalar(ti[:, :, :], ti[:, :, :], LO - 1, None, ALU.bitwise_and))
                v.tensor_copy(kb[:, :, f + 1, :], ti[:, :, :])
                st.run(v.tensor_tensor(kb[:, :, f, :], node, ti[:, :, :], ALU.subtract))
            dve.wait_ge(acts, 3)
            st.run(v.scalar_tensor_tensor(z[:, :, :], z[:, :, :], 0.0, a[:, :, :], ALU.max, ALU.add))
            st.run(v.tensor_tensor(z[:, :, :], z[:, :, :], kf[:, :, :, 1], ALU.mult))
            st.run(v.tensor_tensor(b[:, :, :], kf[:, :, :, 0], kf[:, :, :, 3], ALU.not_equal))
            v.tensor_tensor(kf[:, :, :, 2], z[:, :, :], b[:, :, :], ALU.mult)
            v.tensor_scalar(kf[:, :, :, 1], kf[:, :, :, 1], 0.2, None, ALU.mult)


def count_edges(c, KB, start):
    nc = c.nc
    made, free, counted, step, moved, pre = (
        c.sem(n) for n in ("hot_made", "hot_free", "all_counted", "count_step", "count_moved", "rows_before"))
    with ExitStack() as local:
        def sb(name, shape, dt=F32):
            return local.enter_context(nc.sbuf_tensor(name, shape, dt))

        hot_lo = [sb(f"hot_lo{s}", [P, T, LO], BF16) for s in range(2)]
        hot_hi = [sb(f"hot_hi{s}", [P, T, HI], BF16) for s in range(2)]
        zb = sb("zb", [P, P], BF16)
        many = sb("many", [HI, LO])
        upto = sb("upto", [HI, LO])
        rows = sb("rows", [HI, 1])
        end = sb("end", [P, NJ])
        t0, t1 = sb("node_t0", [P, NJ]), sb("node_t1", [P, NJ])
        hist = local.enter_context(nc.psum_tensor("hist", [P, 512], F32))
        before = local.enter_context(nc.psum_tensor("before", [P, 512], F32))
        block = local.enter_context(nc.Block())

        @block.vector
        def _(dve):
            v = nc.vector
            st = Steps(dve, step)
            st.done(v.memset(zb[:, :], 0.0))
            with dve.Fori(0, UNITS // 2) as i:
                for s in range(2):
                    dve.wait_ge(free, 2 * i + s + 1)
                    u = (2 * i + s) * 16
                    v.tensor_tensor(hot_hi[s][:, :, :], spread(KB[:, bass.ds(u, T)], HI),
                                    spread_mid(c.count_hi[:, :], T), ALU.is_equal)
                    v.tensor_tensor(hot_lo[s][:, :, :], spread(KB[:, bass.ds(u + T, T)], LO),
                                    spread_mid(c.count_lo[:, :], T), ALU.is_equal).then_inc(made, 1)
            dve.wait_ge(counted, 1)
            st.run(v.tensor_copy(many[:, :], hist[0:HI, 0:LO]))
            st.run(v.tensor_tensor_scan(upto[:, :], c.ones[0:HI, :], many[:, :], 0.0, ALU.mult, ALU.add))
            dve.wait_ge(pre, 1)
            st.run(v.tensor_copy(rows[:, :], before[0:HI, 0:1]))
            st.run(v.tensor_tensor(upto[:, :], upto[:, :], many[:, :], ALU.subtract))
            st.run(v.tensor_scalar(start[:, :], upto[:, :], rows[:, 0:1], None, ALU.add))
            dve.wait_ge(moved, 64)
            cnt, off = c.cnt[:, :], c.off[:, :]
            v.tensor_scalar(c.has[:, :], cnt, 0.0, None, ALU.is_gt)
            v.tensor_scalar(c.keep[:, :], c.spare_pos[:, :], float(EP + N), None, ALU.is_ge)
            st.run(v.tensor_tensor(end[:, :], off, cnt, ALU.add))
            st.run(v.tensor_tensor(t0[:, :], off, c.spare_pos[:, :], ALU.subtract))
            v.tensor_tensor(c.keep[:, :], c.keep[:, :], c.has[:, :], ALU.max)
            st.run(v.tensor_tensor(t0[:, :], t0[:, :], c.has[:, :], ALU.mult))
            v.tensor_tensor(c.first[:, :], t0[:, :], c.spare_pos[:, :], ALU.add)
            st.run(v.tensor_scalar(t1[:, :], end[:, :], -1.0, None, ALU.add))
            v.tensor_tensor(c.last[:, :], t1[:, :], c.has[:, :], ALU.mult)
            st.run(v.tensor_scalar(t0[:, :], end[:, :], float(HALF), None, ALU.is_gt))
            v.scalar_tensor_tensor(c.cross[:, :], off, float(HALF), t0[:, :], ALU.is_lt, ALU.mult)
            v.scalar_tensor_tensor(c.middle[:, :], off, float(HALF), t0[:, :], ALU.is_le, ALU.mult)

        @block.tensor
        def _(pe):
            t = nc.tensor
            pe.sem_inc(free, 2)
            pe.wait_ge(step, 1)
            h = hist[0:HI, 0:LO]
            t.matmul(h, zb[:, 0:HI], zb[:, 0:LO], start=True, stop=True)
            with pe.Fori(0, UNITS // 2) as i:
                for s in range(2):
                    pe.wait_ge(made, 2 * i + s + 1)
                    for k in range(T):
                        mm = t.matmul(h, hot_hi[s][:, k, :], hot_lo[s][:, k, :], start=False, stop=True,
                                      skip_group_check=True)
                    mm.then_inc(free, 1)
            t.matmul(h, zb[:, 0:HI], zb[:, 0:LO], start=False, stop=True, skip_group_check=True)\
                .then_inc(counted, 1)
            pe.wait_ge(step, 3)
            t.matmul(before[0:HI, 0:1], c.above[0:HI, 0:HI], upto[:, LO - 1:LO], start=True, stop=True)\
                .then_inc(pre, 1)

        @block.sync
        def _(sp):
            sp.wait_ge(step, 6)
            sp.dma_start(c.start_dram.rearrange("(h l) -> h l", l=LO), start[:, :]).then_inc(moved, 16)
            sp.dma_start(c.count_dram.rearrange("(h l) -> h l", l=LO), many[:, :]).then_inc(moved, 16)
            sp.wait_ge(moved, 32)
            sp.dma_start(c.off[:, :], c.start_dram.rearrange("(p j) -> p j", p=P)).then_inc(moved, 16)
            sp.dma_start(c.cnt[:, :], c.count_dram.rearrange("(p j) -> p j", p=P)).then_inc(moved, 16)


def sort_and_aggregate(c, KF, KB, start):
    nc = c.nc
    names = ("attr_in0", "attr_in1", "rec_in0", "rec_in1", "staged", "rec_filled", "rows_up", "hi_up", "picked",
             "picks_read", "added", "hist_copied", "same_made", "summed", "sums_copied", "place_made",
             "rec_out0", "rec_out1", "sort_step", "rows_read", "hi_read", "pads_in", "pads_zero",
             "rows_zero", "sync_waited", "pool_waited")
    S = {n: c.sem(n) for n in names}
    tables_out = [c.sem(f"table_out{t}") for t in range(TABLES)]
    start_at_one(c, [sem for name, sem in S.items() if not name.startswith("rec_out")])
    with ExitStack() as local:
        def sb(name, shape, dt=F32):
            return local.enter_context(nc.sbuf_tensor(name, shape, dt))

        def ps(name):
            return local.enter_context(nc.psum_tensor(name, [P, 512], F32))

        attr = [sb(f"attr{s}", [P, T, D + 1]) for s in range(2)]
        rec = [sb(f"rec{s}", [P, T, RW]) for s in range(2)]
        kb = [sb(f"kb{s}", [P, 4, T], BF16) for s in range(2)]
        kf = [sb(f"kf{s}", [P, T, 4]) for s in range(2)]
        hot_lo = [sb(f"shot_lo{s}", [P, T, LO], BF16) for s in range(2)]
        hot_hi = [sb(f"shot_hi{s}", [P, T, HI], BF16) for s in range(2)]
        pick = [sb(f"pick{s}", [HI, UE]) for s in range(2)]
        same = sb("same_dst", [P, T, P])
        sums = [sb(f"sums{s}", [P, T, D + 1]) for s in range(2)]
        table = [sb(f"hist_now{k}", [HI, LO]) for k in range(2)]
        rank, base, dup, t0 = (sb(n, [P, T]) for n in ("rank", "base", "dup", "srt0"))
        junk_dup, junk_rank, junk_pick = (sb(f"junk{n}", [P, T, P]) for n in range(3))
        zeros = sb("row_zeros", [P, T * HID])
        place = [sb(f"place{s}", [P, T], I32) for s in range(2)]
        row = [sb(f"row{s}", [P, T], I32) for s in range(2)]
        src_row, dst_row, hi_row, picks, hist, total = (
            ps(n) for n in ("src_row", "dst_row", "hi_row", "picks", "hist2", "total"))
        block = local.enter_context(nc.Block())
        attr_dram = c.edge_attr_64
        small = c.edge_attr_16

        @block.sync
        def _(sp):
            def load(u, s):
                sp.dma_start(attr[s][:, :, 0:D], attr_dram[bass.ds(u * UE, UE), :]
                             .rearrange("(p k) d -> p k d", k=T)).then_inc(S[f"attr_in{s}"], 16)
                sp.dma_start(rec[s][:, :, 0:DE], small[bass.ds(u * UE, UE), :]
                             .rearrange("(p k) d -> p k d", k=T)).then_inc(S[f"rec_in{s}"], 16)

            def fill(u):
                for table, w in ((c.src_rows, D), (c.src_wide, HID)):
                    sp.dma_start(table[bass.ds(u * UE, UE), :].rearrange("(p k) d -> p (k d)", p=P),
                                 zeros[:, 0:T * w]).then_inc(S["rows_zero"], 16)

            def freed(i, s):
                sp.wait_ge(S["summed"], 2 * i + s + 1)
                waited(sp, S["sync_waited"])
                if used(i):
                    sp.wait_ge(S[f"rec_out{s}"], 64 * i)
                waited(sp, S["sync_waited"])
            sp.wait_ge(S["pads_zero"], 2)
            def pair(i):
                for s in range(2):
                    freed(i, s)
                    load(2 * i + s, s)
                    fill(2 * i + s)

            from_zero(sp, pair, FULL // 2)
            assert FULL % 2 == 0 and RESTK
            i = FULL // 2
            for s in range(2):
                freed(i, s)
            sp.wait_ge(S["pads_zero"], 1 + 3)
            for buf, dram, w, sem in ((attr[0], attr_dram, D, "attr_in0"), (rec[0], small, DE, "rec_in0")):
                sp.dma_start(buf[0:RESTP, :, 0:w], dram[FULL * UE:FULL * UE + RESTP * T, :]
                             .rearrange("(p k) d -> p k d", k=T)).then_inc(S["pads_in"], 16)
                sp.dma_start(buf[RESTP:RESTP + 1, 0:RESTK, 0:w], dram[E - RESTK:E, :]
                             .rearrange("(p k) d -> p k d", p=1)).then_inc(S["pads_in"], 16)
            for s in range(2):
                fill(2 * i + s)
            sp.wait_ge(S["rows_zero"], 32 * UNITS + 1)
            sp.wait_ge(S["pads_in"], 65)
            for sem in ("attr_in0", "rec_in0", "attr_in1", "rec_in1"):
                sp.sem_inc(S[sem], 16)

        @block.scalar
        def _(act):
            a = nc.scalar
            act.wait_ge(S["added"], 2)
            a.copy(table[0][:, :], hist[0:HI, 0:LO]).then_inc(S["hist_copied"], 1)
            def pair(i):
                for s in range(2):
                    u = 2 * i + s
                    act.wait_ge(S["place_made"], u + 2)
                    a.copy(kb[s][:, :, :], KB[:, bass.ds(u * 16, 16)].rearrange("p (f k) -> p f k", f=4))
                    a.copy(kf[s][:, :, :], KF[:, bass.ds(u * 16, 16)].rearrange("p (k f) -> p k f", f=4))\
                        .then_inc(S["staged"], 1)
                    act.wait_ge(S["staged"], u + 2)
                    if used(i):
                        act.wait_ge(S[f"rec_out{s}"], 64 * i)
                    a.copy(rec[s][:, :, DE:DE + 3], kf[s][:, :, 1:4]).then_inc(S["rec_filled"], 1)
                    for k in range(T):
                        act.wait_ge(S["added"], T * u + k + 3)
                        act.wait_ge(S["picked"], T * u + k + 1)
                        a.copy(table[(k + 1) % 2][:, :], hist[0:HI, 0:LO]).then_inc(S["hist_copied"], 1)
                    act.wait_ge(S["summed"], u + 3)
                    for k in range(T):
                        if used(i):
                            act.wait_ge(tables_out[T * s + k], 16 * i)
                    a.copy(sums[s][:, :, :], total[:, 0:T * (D + 1)].rearrange("p (k d) -> p k d", k=T))\
                        .then_inc(S["sums_copied"], 1)

            from_zero(act, pair, UNITS // 2)

        @block.tensor
        def _(pe):
            t = nc.tensor
            h = hist[0:HI, 0:LO]
            pe.sem_inc(S["summed"], 1)
            t.matmul(h, c.ident[0:HI, 0:HI], start[:, :], start=True, stop=True).then_inc(S["added"], 1)
            def pair(i):
                for s in range(2):
                    u = 2 * i + s
                    pe.wait_ge(S["staged"], u + 2)
                    pe.wait_ge(S["hi_read"], u + 2)
                    for k in range(T):
                        col = slice(k * P, (k + 1) * P)
                        mm = t.matmul(hi_row[:, col], kb[s][:, 0, k:k + 1].to_broadcast([P, P]), c.identb[:, :],
                                      start=True, stop=True)
                    mm.then_inc(S["hi_up"], 1)
                    pe.wait_ge(S["rows_read"], u + 2)
                    for f, rows in ((0, src_row), (2, dst_row)):
                        for k in range(T):
                            col = slice(k * P, (k + 1) * P)
                            for g in range(2):
                                mm = t.matmul(rows[:, col], kb[s][:, f + g, k:k + 1].to_broadcast([P, P]),
                                              c.identb[:, :], start=(g == 0), stop=(g == 1))
                    mm.then_inc(S["rows_up"], 1)
                    pe.wait_ge(S["hi_read"], u + 3)
                    pe.wait_ge(S["picks_read"], u + 2)
                    for k in range(T):
                        pe.wait_ge(S["hist_copied"], T * u + k + 2)
                        t.matmul(picks[:, k * LO:(k + 1) * LO], pick[s][:, k * P:(k + 1) * P],
                                 table[k % 2][:, :], start=True, stop=True).then_inc(S["picked"], 1)
                        t.matmul(h, hot_hi[s][:, k, :], hot_lo[s][:, k, :], start=False, stop=True,
                                 skip_group_check=True).then_inc(S["added"], 1)
                    pe.wait_ge(S["same_made"], u + 2)
                    pe.wait_ge(S[f"attr_in{s}"], 16 * (i + 1) + 1)
                    pe.wait_ge(S["sums_copied"], u + 1)
                    for k in range(T):
                        mm = t.matmul(total[:, k * (D + 1):(k + 1) * (D + 1)], same[:, k, :], attr[s][:, k, :],
                                      start=True, stop=True)
                    mm.then_inc(S["summed"], 1)

            from_zero(pe, pair, UNITS // 2)

        @block.vector
        def _(dve):
            v = nc.vector
            PER = 3
            v.memset(zeros[:, :], 0.0)
            for s in range(2):
                v.memset(attr[s][:, :, :], 0.0)
                v.memset(rec[s][:, :, :], 0.0)
            v.memset(junk_dup[:, 0, :], 0.0).then_inc(S["sort_step"], 1)
            dve.wait_ge(S["sort_step"], 2)
            for s in range(2):
                last = v.memset(attr[s][:, :, D:D + 1], 1.0)
            last.then_inc(S["pads_zero"], 1)
            dve.sem_inc(S["hi_read"], 1)
            dve.sem_inc(S["rows_read"], 1)
            dve.sem_inc(S["picks_read"], 1)
            dve.sem_inc(S["place_made"], 2)

            def unit(i, s):
                u = 2 * i + s
                st = Steps(dve, S["sort_step"], 2 + PER * u)
                dve.wait_ge(S["staged"], u + 2)
                v.tensor_tensor(hot_hi[s][:, :, :], spread(kb[s][:, 0, :], HI), spread_mid(c.count_hi[:, :], T),
                                ALU.is_equal)
                v.tensor_tensor(hot_lo[s][:, :, :], spread(kb[s][:, 1, :], LO), spread_mid(c.count_lo[:, :], T),
                                ALU.is_equal)
                dve.wait_ge(S["hi_up"], u + 2)
                v.tensor_scalar(pick[s][:, :], hi_row[0:HI, :], c.part_hi[0:HI, 0:1], None, ALU.is_equal)\
                    .then_inc(S["hi_read"], 1)
                dve.wait_ge(S["rows_up"], u + 2)
                dve.wait_ge(S["summed"], u + 2)
                v.tensor_tensor(same[:, :, :], dst_row[:, :].rearrange("p (k e) -> p k e", k=T),
                                spread(kf[s][:, :, 3], P), ALU.is_equal).then_inc(S["same_made"], 1)
                dve.wait_ge(S["same_made"], u + 2)
                for k in range(T):
                    v.tensor_tensor_reduce(junk_dup[:, k, :], same[:, k, :], c.below[:, :], 1.0, 0.0, ALU.mult, ALU.add,
                                           dup[:, k:k + 1])
                    last = v.scalar_tensor_tensor(junk_rank[:, k, :], src_row[:, k * P:(k + 1) * P], kf[s][:, k, 0:1],
                                                  c.below[:, :], ALU.is_equal, ALU.mult,
                                                  accum_out=rank[:, k:k + 1])
                last.then_inc(S["rows_read"], 1)
                dve.wait_ge(S["rows_read"], u + 3)
                st.run(v.tensor_tensor(t0[:, :], c.spare_row[:, :], kf[s][:, :, 3], ALU.subtract))
                st.run(v.scalar_tensor_tensor(t0[:, :], dup[:, :], 0.0, t0[:, :], ALU.is_gt, ALU.mult))
                for k in range(T):
                    if used(i):
                        dve.wait_ge(tables_out[T * s + k], 16 * i)
                st.run(v.tensor_tensor(row[s][:, :], t0[:, :], kf[s][:, :, 3], ALU.add))
                dve.wait_ge(S["picked"], T * (u + 1) + 1)
                for k in range(T):
                    last = v.tensor_tensor_reduce(junk_pick[:, k, 0:LO], picks[:, k * LO:(k + 1) * LO], hot_lo[s][:, k, :],
                                                  1.0, 0.0, ALU.mult, ALU.add, base[:, k:k + 1])
                last.then_inc(S["picks_read"], 1)
                dve.wait_ge(S["picks_read"], u + 3)
                if used(i):
                    dve.wait_ge(S[f"rec_out{s}"], 64 * i)
                v.tensor_tensor(place[s][:, :], rank[:, :], base[:, :], ALU.add).then_inc(S["place_made"], 1)
                assert st.n == PER

            def pair(i):
                for s in range(2):
                    unit(i, s)

            from_zero(dve, pair, FULL // 2)
            i = FULL // 2
            dve.wait_ge(S["summed"], 2 * i + 2)
            for s in range(2):
                if used(i):
                    dve.wait_ge(S[f"rec_out{s}"], 64 * i)
                v.memset(attr[s][:, :, 0:D], 0.0)
                v.memset(rec[s][:, :, 0:DE], 0.0).then_inc(S["pads_zero"], 1)
            for s in range(2):
                unit(i, s)

        @block.gpsimd
        def _(pool):
            def pair(i):
                for s in range(2):
                    u = 2 * i + s
                    pool.wait_ge(S["sums_copied"], u + 2)
                    pool.wait_ge(S["place_made"], u + 4)
                    pool.wait_ge(S["rec_filled"], u + 2)
                    pool.wait_ge(S[f"rec_in{s}"], 16 * (i + 1) + 1)
                    for k in range(T):
                        if used(i):
                            pool.wait_ge(tables_out[T * s + k], 16 * i)
                    waited(pool, S["pool_waited"])
                    for k in range(T):
                        n = T * s + k
                        nc.gpsimd.indirect_dma_start(
                            c.agg_parts[n], bass.IndirectOffsetOnAxis(row[s][:, k:k + 1], 0), sums[s][:, k, :],
                            None, compute_op=ALU.add).then_inc(tables_out[n], 16)
                        nc.gpsimd.indirect_dma_start(
                            c.records, bass.IndirectOffsetOnAxis(place[s][:, k:k + 1], 0), rec[s][:, k, :],
                            None).then_inc(S[f"rec_out{s}"], 16)

            from_zero(pool, pair, UNITS // 2)
            for n in range(TABLES):
                pool.wait_ge(tables_out[n], 16 * UNITS // 2)
            for s in range(2):
                pool.wait_ge(S[f"rec_out{s}"], 64 * UNITS // 2)


def normalise(c, h, sems, total):
    nc = c.nc
    step, rooted = sems
    with ExitStack() as local:
        t = local.enter_context(nc.sbuf_tensor(c.fresh("ln_t"), [P, NJ, D], F32))
        m, r = (local.enter_context(nc.sbuf_tensor(c.fresh(n), [P, NJ], F32)) for n in ("ln_m", "ln_r"))
        block = local.enter_context(nc.Block())
        base = total * 8

        @block.vector
        def _(dve):
            v = nc.vector
            st = Steps(dve, step, base)
            st.run(v.tensor_reduce(m[:, :], c.xs[:, :, :], AX_X, ALU.add))
            st.run(v.tensor_scalar(m[:, :], m[:, :], 1.0 / D, None, ALU.mult))
            st.run(v.tensor_tensor(h[:, :, :], c.xs[:, :, :], spread(m[:, :], D), ALU.subtract))
            st.run(v.tensor_tensor(t[:, :, :], h[:, :, :], h[:, :, :], ALU.mult))
            st.run(v.tensor_reduce(r[:, :], t[:, :, :], AX_X, ALU.add))
            st.run(v.tensor_scalar(r[:, :], r[:, :], 1.0 / D, LN_EPS, ALU.mult, ALU.add))
            dve.wait_ge(rooted, total + 1)
            st.run(v.reciprocal(r[:, :], m[:, :]))
            st.run(v.scalar_tensor_tensor(h[:, :, :], h[:, :, :], 0.0, spread(r[:, :], D), ALU.max, ALU.mult))

        @block.scalar
        def _(act):
            act.wait_ge(step, base + 6)
            nc.scalar.activation(m[:, :], r[:, :], ACT.Sqrt).then_inc(rooted, 1)


def project(c, h, w, bias, out, width):
    nc = c.nc
    turned, taken, made, kept = c.project_sems
    base = c.projected * NB
    c.projected += 1
    with ExitStack() as local:
        up = [local.enter_context(nc.psum_tensor(c.fresh("pj_up"), [P, 512], F32)) for _ in range(2)]
        res = [local.enter_context(nc.psum_tensor(c.fresh("pj_res"), [P, 512], F32)) for _ in range(2)]
        ht = [local.enter_context(nc.sbuf_tensor(c.fresh("pj_ht"), [D, 4 * P], F32)) for _ in range(2)]
        block = local.enter_context(nc.Block())

        @block.tensor
        def _(pe):
            def turn(b):
                if b >= 2:
                    pe.wait_ge(taken, base + b - 1)
                for k in range(4):
                    mm = nc.tensor.transpose(up[b % 2][0:D, k * P:(k + 1) * P], h[:, 4 * b + k, :], c.ident[:, :])
                mm.then_inc(turned, 1)

            turn(0)
            for b in range(NB):
                if b + 1 < NB:
                    turn(b + 1)
                pe.wait_ge(taken, base + b + 1)
                if b >= 2:
                    pe.wait_ge(kept, base + b - 1)
                for k in range(4):
                    mm = nc.tensor.matmul(res[b % 2][:, k * width:(k + 1) * width], ht[b % 2][:, k * P:(k + 1) * P],
                                          w, start=True, stop=True)
                mm.then_inc(made, 1)

        @block.scalar
        def _(act):
            for b in range(NB):
                act.wait_ge(turned, base + b + 1)
                if b >= 2:
                    act.wait_ge(made, base + b - 1)
                nc.scalar.copy(ht[b % 2][:, :], up[b % 2][0:D, :]).then_inc(taken, 1)

        @block.vector
        def _(dve):
            for b in range(NB):
                dve.wait_ge(made, base + b + 1)
                r = res[b % 2][:, 0:4 * width].rearrange("p (k f) -> p k f", k=4)
                nc.vector.tensor_tensor(out[:, 4 * b:4 * b + 4, :], r, spread_mid(bias, 4), ALU.add).then_inc(kept, 1)


def load_all(c, pairs):
    nc = c.nc
    base = c.loads
    c.loads += 16 * len(pairs)
    with nc.Block() as block:
        @block.sync
        def _(sp):
            for dst, src in pairs:
                sp.dma_start(dst, src, allow_slow_non_contiguous=True).then_inc(c.load_sem, 16)
            sp.wait_ge(c.load_sem, base + 16 * len(pairs))


def place_rows(c, rows, width, table, spots, marks=None, table_rows=None):
    nc = c.nc
    base, sbase, pbase = c.placed, c.spotted, c.middles
    split = spots is c.src_rows
    c.placed += 16
    c.spotted += 16 * NJ * (2 if marks is not None else 1)
    with ExitStack() as local:
        acc = local.enter_context(nc.psum_tensor(c.fresh("mid_ps"), [P, 512], F32))
        mid = local.enter_context(nc.sbuf_tensor(c.fresh("mid_row"), [1, width], F32))
        block = local.enter_context(nc.Block())
        if split:
            c.middles += 1
            c.placed += 16

        @block.sync
        def _(sp):
            if table is not None:
                sp.dma_start(table.rearrange("(p j) d -> p j d", p=P),
                             rows if table_rows is None else table_rows).then_inc(c.place_sem, 16)
                sp.wait_ge(c.place_sem, base + 16)
            else:
                sp.sem_inc(c.place_sem, 16)
            if split:
                sp.wait_ge(c.middle_sem, 2 * pbase + 2)
                sp.wait_ge(c.spot_sem, c.spotted)
                sp.dma_start(spots[HALF:HALF + 1, :], mid[:, :]).then_inc(c.place_sem, 16)
                sp.wait_ge(c.place_sem, base + 32)

        @block.gpsimd
        def _(pool):
            for j in range(NJ):
                nc.gpsimd.indirect_dma_start(spots, bass.IndirectOffsetOnAxis(c.first[:, j:j + 1], 0),
                                             rows[:, j, :], None).then_inc(c.spot_sem, 16)
                if marks is not None:
                    nc.gpsimd.indirect_dma_start(c.same, bass.IndirectOffsetOnAxis(c.first[:, j:j + 1], 0),
                                                 marks, None).then_inc(c.spot_sem, 16)
            pool.wait_ge(c.spot_sem, c.spotted)

        if split:
            @block.tensor
            def _(pe):
                for j in range(NJ):
                    mm = nc.tensor.matmul(acc[0:1, 0:width], c.middle[:, j:j + 1], rows[:, j, :], start=(j == 0),
                                          stop=(j == NJ - 1))
                mm.then_inc(c.middle_sem, 1)

            @block.vector
            def _(dve):
                dve.wait_ge(c.middle_sem, 2 * pbase + 1)
                nc.vector.tensor_copy(mid[:, :], acc[0:1, 0:width]).then_inc(c.middle_sem, 1)


def fetch_ends(c, seg, width, agg, carry):
    nc = c.nc
    base = c.carried
    c.fetched += 16 * NJ
    c.carried += 16 if carry is not None else 0
    with nc.Block() as block:
        @block.gpsimd
        def _(pool):
            for j in range(NJ):
                nc.gpsimd.indirect_dma_start(agg[:, j, :], None, seg,
                                             bass.IndirectOffsetOnAxis(c.last[:, j:j + 1], 0)).then_inc(c.fetch_sem, 16)
            pool.wait_ge(c.fetch_sem, c.fetched)

        @block.sync
        def _(sp):
            if carry is not None:
                sp.dma_start(carry, seg[HALF - 1, :].partition_broadcast(P)).then_inc(c.carry_sem, 16)
                sp.wait_ge(c.carry_sem, base + 16)


def unpack_records(c, coupling):
    nc = c.nc
    CU = UNITS // 4
    with ExitStack() as local:
        buf = [local.enter_context(nc.sbuf_tensor(f"unpack{s}", [P, CU, T * RW], F32)) for s in range(2)]
        came = [c.sem(f"unpack_in{s}") for s in range(2)]
        done = c.sem("unpacked")
        block = local.enter_context(nc.Block())

        @block.sync
        def _(sp):
            for n in range(4):
                if n >= 2:
                    sp.wait_ge(done, n)
                sp.dma_start(buf[n % 2][:, :, :], c.records[n * CU * UE:(n + 1) * CU * UE, :]
                             .rearrange("(u p k) f -> p u (k f)", u=CU, p=P)).then_inc(came[n % 2], 16)

        @block.vector
        def _(dve):
            nc.vector.memset(c.dsti[:, UNITS * T:], 0)
            nc.vector.memset(coupling[:, UNITS * T:], 0.0).then_inc(done, 1)
            for n in range(4):
                dve.wait_ge(came[n % 2], 16 * (n // 2 + 1))
                r = buf[n % 2][:, :, :].rearrange("p u (k f) -> p u k f", k=T)
                at = slice(n * CU * T, (n + 1) * CU * T)
                nc.vector.tensor_copy(c.dsti[:, at].rearrange("p (u k) -> p u k", k=T), r[:, :, :, 18])
                nc.vector.tensor_copy(coupling[:, at].rearrange("p (u k) -> p u k", k=T), r[:, :, :, 17])\
                    .then_inc(done, 1)


def spread_marks(table, g):
    return table[0:EP, :].rearrange("(h e) o -> h (e o)", h=2)[:, bass.ds(g * UE, UE)].unsqueeze(1)\
        .to_broadcast([2, 64, UE])


def group_rows(table, g):
    return table.rearrange("(h e) d -> h e d", h=2)[:, bass.ds(g * UE, UE), :]\
        .rearrange("h (p k) d -> p h (k d)", k=T)


class Turn:

    def __init__(self, q, s):
        self.q, self.s, self.n = q, s, 2 * q + s

    def __add__(self, d):
        return Turn(self.q + (self.s + d) // 2, (self.s + d) % 2)

    def __sub__(self, d):
        return self + -d


def turns(eng, body, first, loops, last):
    with eng.Fori(0, loops) as i:
        body(Turn(i, 0) + first)
        body(Turn(i, 0) + (first + 1))
    for g in range(first + 2 * loops, last):
        body(Turn(g // 2, g % 2))


def layer0_edges(c, coupling, mixes):
    nc = c.nc
    names = ("pool_waited", "sync_waited", "staged",
             "t_up", "filled", "prodded", "squared", "sums_up", "rooted", "weights_made", "weights_up",
             "weighted", "seg_made", "out_up", "out_copied", "gathered0", "gathered1", "rows_in0", "rows_in1",
             "fm_in0", "fm_in1", "sm_in0", "sm_in1", "stored0", "stored1", "step", "b_kept", "norms_kept",
             "coupled")
    S = {n: c.sem("l0_" + n) for n in names}
    start_at_one(c, [sem for name, sem in S.items() if not name.startswith("gathered")])
    LOOPS = (HU - 4) // 2
    with ExitStack() as local:
        def sb(name, shape, dt=F32):
            return local.enter_context(nc.sbuf_tensor("l0_" + name, shape, dt))

        def two(name, shape, dt=F32):
            return [sb(f"{name}{s}", shape, dt) for s in range(2)]

        idx = two("idx", [P, T, 2], I32)
        cpl, rt, norm = two("cpl", [P, T, 2]), two("rt", [P, T * 2]), two("norm", [P, T, 2])
        q = two("q", [P, T, 2 * (D + 1)])
        vr, wide, ob = two("vr", [P, T, 2, D]), two("wide", [P, T, 2, D]), two("ob", [P, 2, T, D])
        fm, sm, a, a2, b, prod, seg = (two(n, [P, UE]) for n in ("fm", "sm", "a", "a2", "b", "prod", "seg"))
        den, rcp, sim, pos, mix, wgt = (sb(n, [P, T * 2]) for n in ("den", "rcp", "sim", "pos", "mix", "wgt"))
        msg = sb("msg", [P, UE])
        halves = sb("halves", [P, 2])
        wt, ot = (local.enter_context(nc.psum_tensor("l0_p" + n, [P, UE], F32)) for n in ("wt", "ot"))
        qt, vt, sums_ps = ([local.enter_context(nc.psum_tensor(f"l0_{n}{s}", [P, UE], F32)) for s in range(2)]
                           for n in ("qt", "vt", "sums"))
        block = local.enter_context(nc.Block())

        def by_tile(ap):
            return ap.rearrange("p (e k) -> p k e", k=T)

        @block.sync
        def _(sp):
            def rows_and_marks(g):
                if used(g.q):
                    sp.wait_ge(S["t_up"], g.n + 1)
                    waited(sp, S["sync_waited"])
                for h in range(2):
                    sp.dma_start(vr[g.s][:, :, h, :], c.src_rows[bass.ds(g.n * UE + h * HALF, UE), :]
                                 .rearrange("(p k) d -> p k d", k=T)).then_inc(S[f"rows_in{g.s}"], 16)
                if used(g.q):
                    sp.wait_ge(S["filled"], g.n + 1)
                    waited(sp, S["sync_waited"])
                marks(fm, g, "fm_in")

            def marks(buf, g, sem):
                sp.dma_start(buf[g.s][:, :], spread_marks(c.same, g.n)).then_inc(S[f"{sem}{g.s}"], 16)

            def body(g):
                rows_and_marks(g)
                if used((g - 1).q):
                    sp.wait_ge(S["seg_made"], g.n)
                    waited(sp, S["sync_waited"])
                marks(sm, g - 1, "sm_in")

            zero = Turn(0, 0)
            rows_and_marks(zero)
            body(zero + 1)
            body(zero + 2)
            turns(sp, body, 3, LOOPS - 1, HU)
            sp.wait_ge(S["seg_made"], HU + 1)
            marks(sm, Turn(HU // 2 - 1, 1), "sm_in")

        @block.gpsimd
        def _(pool):
            with pool.Fori(0, HU // 2) as i:
                for s in range(2):
                    g = 2 * i + s
                    pool.wait_ge(S["staged"], g + 2)
                    pool.wait_ge(S["t_up"], g + 1)
                    pool.wait_ge(S["norms_kept"], g + 1)
                    waited(pool, S["pool_waited"])
                    for h in range(2):
                        for k in range(T):
                            nc.gpsimd.indirect_dma_start(
                                q[s][:, k, h * (D + 1):(h + 1) * (D + 1)], None, c.normed_rows[h],
                                bass.IndirectOffsetOnAxis(idx[s][:, k, h:h + 1], 0)).then_inc(S[f"gathered{s}"], 16)

        @block.tensor
        def _(pe):
            t = nc.tensor
            pe.sem_inc(S["t_up"], 1)

            def turn(g):
                pe.wait_ge(S[f"gathered{g.s}"], 128 * (g.q + 1))
                pe.wait_ge(S[f"rows_in{g.s}"], 32 * (g.q + 1) + 1)
                if used(g.q):
                    pe.wait_ge(S["prodded"], g.n)
                for k in range(T):
                    t.transpose(by_tile(qt[g.s][:, :])[:, k, :], q[g.s][:, k, 1:1 + 2 * D], c.ident[:, :])
                for k in range(T):
                    mm = t.transpose(by_tile(vt[g.s][:, :])[:, k, :],
                                     vr[g.s][:, k, :, :].rearrange("p h d -> p (h d)"), c.ident[:, :])
                mm.then_inc(S["t_up"], 1)

            def sums(g):
                pe.wait_ge(S["squared"], g.n + 2)
                pe.wait_ge(S["prodded"], g.n + 2)
                for n, rows in enumerate((a2, prod)):
                    for k in range(T):
                        at = (n * T + k) * 2
                        mm = t.matmul(sums_ps[g.s][:, at:at + 2], by_tile(rows[g.s][:, :])[:, k, :], halves[:, :],
                                      start=True, stop=True)
                mm.then_inc(S["sums_up"], 1)

            def weights(g):
                pe.wait_ge(S["weights_made"], g.n + 2)
                pe.wait_ge(S["weighted"], g.n + 1)
                for k in range(T):
                    mm = t.transpose(by_tile(wt[:, :])[:, k, :],
                                     wide[g.s][:, k, :, :].rearrange("p h d -> p (h d)"), c.ident[:, :])
                mm.then_inc(S["weights_up"], 1)

            def out(g):
                pe.wait_ge(S["seg_made"], g.n + 3)
                pe.wait_ge(S["out_copied"], g.n + 1)
                for k in range(T):
                    mm = t.transpose(ot[:, k * P:(k + 1) * P], by_tile(seg[g.s][:, :])[:, k, :], c.ident[:, :])
                mm.then_inc(S["out_up"], 1)

            zero = Turn(0, 0)
            for g in range(2):
                turn(zero + g)
                sums(zero + g)
            turn(zero + 2)
            weights(zero)

            def body(g, more=True):
                if more:
                    turn(g + 2)
                out(g - 1)
                weights(g)
                sums(g + 1)

            turns(pe, body, 1, LOOPS, HU - 2)
            last = Turn(HU // 2 - 1, 0)
            body(last, more=False)
            weights(last + 1)
            out(last)
            out(last + 1)

        @block.scalar
        def _(act):
            a_ = nc.scalar

            def stage(g):
                for h in range(2):
                    last = a_.copy(idx[g.s][:, :, h], c.dsti[:, bass.ds((g.n + h * HU) * T, T)])
                last.then_inc(S["staged"], 1)

            def couple(g):
                for h in range(2):
                    last = a_.copy(cpl[g.s][:, :, h], coupling[:, bass.ds((g.n + h * HU) * T, T)])
                last.then_inc(S["coupled"], 1)

            def squares(g):
                act.wait_ge(S["t_up"], g.n + 3)
                a_.copy(b[g.s][:, :], qt[g.s][:, :]).then_inc(S["b_kept"], 1)
                act.wait_ge(S["filled"], g.n + 3)
                a_.activation(a2[g.s][:, :], a[g.s][:, :], ACT.Square).then_inc(S["squared"], 1)

            def norms(g):
                a_.copy(norm[g.s][:, :, 0], q[g.s][:, :, 0])
                a_.copy(norm[g.s][:, :, 1], q[g.s][:, :, 2 * D + 1]).then_inc(S["norms_kept"], 1)

            def roots(g):
                act.wait_ge(S["sums_up"], g.n + 2)
                a_.activation(rt[g.s][:, :], sums_ps[g.s][:, 0:T * 2], ACT.Sqrt)\
                    .then_inc(S["rooted"], 1)

            def give(g):
                act.wait_ge(S["out_up"], g.n + 2)
                act.wait_ge(S[f"stored{g.s}"], 16 * g.q + 1)
                a_.copy(ob[g.s][:, :, :, :].rearrange("p h k d -> p k h d"),
                        ot[:, :].rearrange("p (k h d) -> p k h d", k=T, h=2))\
                    .then_inc(S["out_copied"], 1)
                act.wait_ge(S["out_copied"], g.n + 2)
                act.dma_start(group_rows(c.seg_rows, g.n), ob[g.s][:, :, :, :].rearrange("p h k d -> p h (k d)"))\
                   .then_inc(S[f"stored{g.s}"], 16)

            act.sem_inc(S["norms_kept"], 1)
            zero = Turn(0, 0)
            stage(zero)
            stage(zero + 1)
            couple(zero)
            couple(zero + 1)
            for g in range(2):
                act.wait_ge(S[f"gathered{g}"], 128)
                norms(zero + g)
                stage(zero + 2 + g)
                squares(zero + g)
                roots(zero + g)
            act.wait_ge(S["gathered0"], 256)
            stage(zero + 4)
            act.wait_ge(S["weights_made"], 2)
            norms(zero + 2)

            def body(g, feed=True, more=True):
                act.wait_ge(S["weighted"], g.n + 1)
                squares(g + 1)
                couple(g + 1)
                h = g + 2
                if more:
                    act.wait_ge(S[f"gathered{h.s}"], 128 * (h.q + 1))
                if feed:
                    stage(g + 4)
                if more:
                    act.wait_ge(S["weights_made"], g.n + 2)
                    norms(h)
                give(g - 1)
                roots(g + 1)

            turns(act, body, 1, LOOPS - 1, HU - 4)
            for g in range(HU - 4, HU - 1):
                body(Turn(g // 2, g % 2), feed=False, more=g + 2 < HU)
            last = Turn(HU // 2 - 1, 0)
            give(last)
            give(last + 1)
            for s in range(2):
                act.wait_ge(S[f"stored{s}"], 16 * (HU // 2) + 1)

        @block.vector
        def _(dve):
            v = nc.vector
            PER = 6
            v.memset(halves[:, :], 0.0).then_inc(S["filled"], 1)
            dve.wait_ge(S["filled"], 2)
            v.memset(halves[0:64, 0:1], 1.0)
            v.memset(halves[64:128, 1:2], 1.0)
            v.memset(a[1][:, UE - 1:UE], 0.0)
            v.memset(seg[1][:, UE - 1:UE], 0.0).then_inc(S["seg_made"], 1)
            dve.wait_ge(S["seg_made"], 2)

            def fill(g):
                dve.wait_ge(S["t_up"], g.n + 3)
                dve.wait_ge(S[f"fm_in{g.s}"], 16 * (g.q + 1) + 1)
                v.tensor_tensor_scan(a[g.s][:, :], fm[g.s][:, :], vt[g.s][:, :], a[1 - g.s][:, UE - 1:UE], ALU.mult,
                                     ALU.add).then_inc(S["filled"], 1)

            def multiply(g):
                dve.wait_ge(S["filled"], g.n + 3)
                dve.wait_ge(S["b_kept"], g.n + 2)
                v.tensor_tensor(prod[g.s][:, :], a[g.s][:, :], qt[g.s][:, :], ALU.mult).then_inc(S["prodded"], 1)

            def weigh(g):
                st = Steps(dve, S["step"], 1 + PER * g.n)
                dve.wait_ge(S["rooted"], g.n + 2)
                dve.wait_ge(S["coupled"], g.n + 2)
                dve.wait_ge(S["norms_kept"], g.n + 3)
                st.run(v.tensor_tensor(den[:, :], rt[g.s][:, :], norm[g.s][:, :, :].rearrange("p k h -> p (k h)"), ALU.mult))
                st.run(v.tensor_scalar(den[:, :], den[:, :], COS_EPS, None, ALU.max))
                st.run(v.reciprocal(rcp[:, :], den[:, :]))
                st.run(v.tensor_tensor(sim[:, :], rcp[:, :], sums_ps[g.s][:, T * 2:T * 4], ALU.mult))
                st.run(v.tensor_scalar(pos[:, :], sim[:, :], 0.0, mixes[:, 3:4], ALU.max, ALU.mult))
                st.run(v.scalar_tensor_tensor(mix[:, :], sim[:, :], mixes[:, 1:2], pos[:, :], ALU.mult, ALU.add))
                assert st.n == PER
                v.tensor_tensor(wide[g.s][:, :, :, :].rearrange("p k h d -> p (k h) d"), spread(mix[:, :], D),
                                spread(cpl[g.s][:, :, :].rearrange("p k h -> p (k h)"), D), ALU.mult)\
                    .then_inc(S["weights_made"], 1)

            def gather_up(g):
                dve.wait_ge(S["weights_up"], g.n + 2)
                v.tensor_tensor(msg[:, :], b[g.s][:, :], wt[:, :], ALU.mult).then_inc(S["weighted"], 1)
                dve.wait_ge(S["weighted"], g.n + 2)
                dve.wait_ge(S["seg_made"], g.n + 2)
                dve.wait_ge(S[f"sm_in{g.s}"], 16 * (g.q + 1) + 1)
                v.tensor_tensor_scan(seg[g.s][:, :], sm[g.s][:, :], msg[:, :], seg[1 - g.s][:, UE - 1:UE], ALU.mult,
                                     ALU.add).then_inc(S["seg_made"], 1)

            zero = Turn(0, 0)
            for g in range(2):
                fill(zero + g)
                multiply(zero + g)
            weigh(zero)

            def body(g):
                gather_up(g - 1)
                fill(g + 1)
                dve.wait_ge(S["weights_made"], g.n + 1)
                weigh(g)
                multiply(g + 1)

            turns(dve, body, 1, LOOPS, HU - 1)
            last = Turn(HU // 2 - 1, 1)
            gather_up(last - 1)
            dve.wait_ge(S["weights_made"], HU - 1 + 1)
            weigh(last)
            gather_up(last)


def normed_tables(c, wh):
    nc = c.nc
    made, rooted, out = (c.sem(n) for n in ("norms_made", "norms_rooted", "normed_out"))
    with ExitStack() as local:
        full = local.enter_context(nc.sbuf_tensor("normed", [P, NJ, D + 2], F32))
        sq = local.enter_context(nc.sbuf_tensor("squares", [P, NJ, D], F32))
        total = local.enter_context(nc.sbuf_tensor("square_sum", [P, NJ], F32))
        block = local.enter_context(nc.Block())

        @block.vector
        def _(dve):
            st = Steps(dve, made)
            st.run(nc.vector.tensor_tensor(sq[:, :, :], wh[:, :, :], wh[:, :, :], ALU.mult))
            st.run(nc.vector.tensor_reduce(total[:, :], sq[:, :, :], AX_X, ALU.add))

        @block.scalar
        def _(act):
            nc.scalar.copy(full[:, :, 1:1 + D], wh[:, :, :])
            act.wait_ge(made, 2)
            nc.scalar.activation(full[:, :, 0], total[:, :], ACT.Sqrt)
            nc.scalar.activation(full[:, :, D + 1], total[:, :], ACT.Sqrt).then_inc(rooted, 1)

        @block.sync
        def _(sp):
            sp.wait_ge(rooted, 1)
            for h in range(2):
                sp.dma_start(c.normed_rows[h].rearrange("(p j) d -> p j d", p=P), full[:, :, h:h + D + 1])\
                    .then_inc(out, 16)
            sp.wait_ge(out, 32)


def layer0(c, w, b, coeff, scale):
    nc = c.nc
    with ExitStack() as local:
        def sb(name, shape, dt=F32):
            return local.enter_context(nc.sbuf_tensor("l0n_" + name, shape, dt))

        h, wh = sb("h", [P, NJ, D]), sb("wh", [P, NJ, D])
        ws, bs = sb("w", [D, D]), sb("b", [P, D])
        mixes, cp, sc, t = sb("mixes", [P, 4]), sb("cp", [P, 3]), sb("sc", [P, 1]), sb("t", [P, 4])
        zero = sb("zero", [P, 1])
        normalise(c, h[:, :, :], c.ln_sems, 0)
        load_all(c, [(ws[:, :], w), (bs[:, :], b.partition_broadcast(P)), (cp[:, :], coeff.partition_broadcast(P)),
                     (sc[:, :], scale.partition_broadcast(P))])
        project(c, h, ws[:, :], bs[:, :], wh, D)
        step, acts = c.sem("mix_step"), c.sem("mix_act")
        with nc.Block() as block:
            @block.vector
            def _(dve):
                v = nc.vector
                st = Steps(dve, step)
                v.memset(zero[:, :], 0.0)
                st.run(v.tensor_reduce(t[:, 0:1], cp[:, :], AX_X, ALU.max))
                st.run(v.tensor_scalar(cp[:, :], cp[:, :], t[:, 0:1], None, ALU.subtract))
                dve.wait_ge(acts, 1)
                st.run(v.tensor_reduce(t[:, 1:2], mixes[:, 0:3], AX_X, ALU.add))
                st.run(v.reciprocal(t[:, 2:3], t[:, 1:2]))
                st.run(v.tensor_scalar(mixes[:, 0:3], mixes[:, 0:3], t[:, 2:3], None, ALU.mult))
                v.tensor_tensor(mixes[:, 3:4], mixes[:, 0:1], mixes[:, 1:2], ALU.subtract)
                dve.wait_ge(acts, 4)
                v.scalar_tensor_tensor(sc[:, :], sc[:, :], 0.0, t[:, 3:4], ALU.max, ALU.add)

            @block.scalar
            def _(act):
                a = nc.scalar
                act.wait_ge(step, 2)
                a.activation(mixes[:, 0:3], cp[:, :], ACT.Exp).then_inc(acts, 1)
                a.activation(t[:, 3:4], sc[:, :], ACT.Abs).then_inc(acts, 1)
                act.wait_ge(acts, 2)
                a.activation(t[:, 3:4], t[:, 3:4], ACT.Exp, scale=-1.0).then_inc(acts, 1)
                act.wait_ge(acts, 3)
                a.activation(t[:, 3:4], t[:, 3:4], ACT.Ln, bias=c.ones[:, 0:1]).then_inc(acts, 1)
        normed_tables(c, wh)
        place_rows(c, wh[:, :, :], D, None, c.src_rows, zero[:, :])
        with ExitStack() as edges:
            coupling = edges.enter_context(nc.sbuf_tensor("coupling", [P, (UNITS + 2) * T], F32))
            unpack_records(c, coupling)
            layer0_edges(c, coupling, mixes)
        agg, carry = h, bs
        fetch_ends(c, c.seg_rows, D, agg, carry[:, :])
        step = c.sem("l0_end")
        tt = sb("tt", [P, NJ, D])
        with nc.Block() as block:
            @block.vector
            def _(dve):
                v = nc.vector
                st = Steps(dve, step)
                st.run(v.tensor_tensor(agg[:, :, :], agg[:, :, :], spread(c.has[:, :], D), ALU.mult))
                st.run(v.tensor_tensor(tt[:, :, :], spread(c.cross[:, :], D), spread_mid(carry[:, :], NJ), ALU.mult))
                st.run(v.tensor_tensor(agg[:, :, :], agg[:, :, :], tt[:, :, :], ALU.add))
                st.run(v.scalar_tensor_tensor(agg[:, :, :], wh[:, :, :], mixes[:, 2:3], agg[:, :, :], ALU.mult,
                                              ALU.add))
                st.run(v.scalar_tensor_tensor(c.xs[:, :, :], agg[:, :, :], sc[:, 0:1], c.xs[:, :, :], ALU.mult,
                                              ALU.add))


def perceptron(c, parts, b0, func, mids, w_out, b_out, more):
    nc = c.nc
    pes, acts, dves = (c.sem(c.fresh("mlp_" + n)) for n in ("pe", "act", "dve"))
    with ExitStack() as local:
        def ps(name):
            return local.enter_context(nc.psum_tensor(c.fresh(name), [P, 512], F32))

        def sb(name, shape):
            return local.enter_context(nc.sbuf_tensor(c.fresh(name), shape, F32))

        up = [ps("mlp_up") for _ in parts]
        flat = [sb("mlp_in", [k, 4 * P]) for _, k, _ in parts]
        hid = [ps("mlp_hid") for _ in range(1 + len(mids))]
        got = [sb("mlp_got", [P, 4 * P]) for _ in hid]
        res = ps("mlp_res")
        t = sb("mlp_t", [P, 4, D])
        n_pe, n_act, n_dve = len(parts) + len(hid) + 1, len(parts) + len(hid), 2
        layers = [(b0, parts[0][2].shape[-1])] + [(b, w.shape[-1]) for w, b in mids]
        block = local.enter_context(nc.Block())

        @block.tensor
        def _(pe):
            for b in range(NB):
                pe.wait_ge(acts, n_act * b)
                for (rows, k, _), to in zip(parts, up):
                    for j in range(4):
                        mm = nc.tensor.transpose(to[0:k, j * P:(j + 1) * P], rows[:, 4 * b + j, :], c.ident[:, :])
                    mm.then_inc(pes, 1)
                for n, (_, m) in enumerate(layers):
                    pe.wait_ge(acts, n_act * b + len(parts) + n)
                    if n == 0:
                        for q, (_, k, w) in enumerate(parts):
                            mm = nc.tensor.matmul(hid[0][0:m, :], w, flat[q][:, :], start=(q == 0),
                                                  stop=(q == len(parts) - 1))
                    else:
                        mm = nc.tensor.matmul(hid[n][0:m, :], mids[n - 1][0], got[n - 1][0:layers[n - 1][1], :],
                                              start=True, stop=True)
                    mm.then_inc(pes, 1)
                pe.wait_ge(acts, n_act * (b + 1))
                pe.wait_ge(dves, n_dve * b)
                for j in range(4):
                    mm = nc.tensor.matmul(res[:, j * D:(j + 1) * D], got[-1][0:layers[-1][1], j * P:(j + 1) * P],
                                          w_out, start=True, stop=True)
                mm.then_inc(pes, 1)

        @block.scalar
        def _(act):
            for b in range(NB):
                for q, (_, k, _) in enumerate(parts):
                    act.wait_ge(pes, n_pe * b + q + 1)
                    nc.scalar.copy(flat[q][:, :], up[q][0:k, :]).then_inc(acts, 1)
                for n, (bias, m) in enumerate(layers):
                    act.wait_ge(pes, n_pe * b + len(parts) + n + 1)
                    nc.scalar.activation(got[n][0:m, :], hid[n][0:m, :], func, bias=bias).then_inc(acts, 1)

        @block.vector
        def _(dve):
            for b in range(NB):
                dve.wait_ge(pes, n_pe * (b + 1))
                x = c.xs[:, 4 * b:4 * b + 4, :]
                st = Steps(dve, dves, n_dve * b)
                st.run(nc.vector.tensor_tensor(t[:, :, :], res[:, 0:4 * D].rearrange("p (j d) -> p j d", j=4),
                                               spread_mid(b_out, 4), ALU.add))
                if more is not None:
                    nc.vector.tensor_tensor(x, x, more[:, 4 * b:4 * b + 4, :], ALU.add).then_inc(c.more_sem, 1)
                    dve.wait_ge(c.more_sem, b + 1)
                st.run(nc.vector.tensor_tensor(x, x, t[:, :, :], ALU.add))


def column(v):
    return v.rearrange("(a o) -> a o", o=1)


def layer1(c, w0, b0, w1, b1, w2, b2):
    nc = c.nc
    with ExitStack() as local:
        def sb(name, shape, dt=F32):
            return local.enter_context(nc.sbuf_tensor("l1_" + name, shape, dt))

        both = sb("both", [P, NJ, 2 * D])
        total = sb("total", [P, NJ, D + 1])
        part = [sb(f"part{s}", [P, NJ, D + 1]) for s in range(2)]
        many = sb("many", [P, NJ])
        w0s, w1s, w2s = sb("w0", [2 * D, D]), sb("w1", [D, D]), sb("w2", [D, D])
        b0s, b1s, b2s = sb("b0", [D, 1]), sb("b1", [D, 1]), sb("b2", [P, D])
        normalise(c, both[:, :, D:2 * D], c.ln_sems, 1)
        load_all(c, [(w0s[:, :], w0), (w1s[:, :], w1), (w2s[:, :], w2), (b0s[:, :], column(b0)),
                     (b1s[:, :], column(b1)), (b2s[:, :], b2.partition_broadcast(P))])
        came, added, step = [c.sem(f"part_in{s}") for s in range(2)], c.sem("part_added"), c.sem("mean_step")
        with nc.Block() as block:
            @block.sync
            def _(sp):
                for t in range(TABLES):
                    if t >= 2:
                        sp.wait_ge(added, t - 1)
                    sp.dma_start(part[t % 2][:, :, :], c.agg_parts[t][0:NP, :].rearrange("(p j) d -> p j d", p=P))\
                        .then_inc(came[t % 2], 16)

            @block.vector
            def _(dve):
                v = nc.vector
                for t in range(TABLES):
                    dve.wait_ge(came[t % 2], 16 * (t // 2 + 1))
                    if t == 0:
                        v.tensor_copy(total[:, :, :], part[0][:, :, :]).then_inc(added, 1)
                    else:
                        v.tensor_tensor(total[:, :, :], total[:, :, :], part[t % 2][:, :, :], ALU.add)\
                            .then_inc(added, 1)
                    dve.wait_ge(added, t + 1)
                st = Steps(dve, step)
                st.run(v.tensor_scalar(many[:, :], total[:, :, D], 1.0, None, ALU.max))
                st.run(v.reciprocal(many[:, :], many[:, :]))
                v.tensor_tensor(both[:, :, 0:D], total[:, :, 0:D], spread(many[:, :], D), ALU.mult)
        perceptron(c, [(both, 2 * D, w0s[:, :])], b0s[:, :], ACT.Relu, [(w1s[:, :], b1s[:, :])], w2s[:, :],
                   b2s[:, :], None)


def layer2_first(c, stats):
    nc = c.nc
    names = ("pool_waited", "sync_waited", "staged",
             "t_up", "filled", "added", "gathered0", "gathered1", "rows_in0", "rows_in1", "fm_in0",
             "fm_in1", "stored0", "stored1")
    S = {n: c.sem("l2_" + n) for n in names}
    start_at_one(c, [sem for name, sem in S.items() if not name.startswith("gathered")])
    LOOPS = (HU - 4) // 2
    with ExitStack() as local:
        def sb(name, shape, dt=F32):
            return local.enter_context(nc.sbuf_tensor("l2_" + name, shape, dt))

        def two(name, shape, dt=F32):
            return [sb(f"{name}{s}", shape, dt) for s in range(2)]

        idx = two("idx", [P, T, 2], I32)
        q, vr = (two(n, [P, T, 2, D]) for n in ("q", "vr"))
        fm, a, u = (two(n, [P, UE]) for n in ("fm", "a", "u"))
        qt, vt = ([local.enter_context(nc.psum_tensor(f"l2_{n}{s}", [P, UE], F32)) for s in range(2)]
                  for n in ("qt", "vt"))
        block = local.enter_context(nc.Block())

        def by_tile(ap):
            return ap.rearrange("p (e k) -> p k e", k=T)

        @block.sync
        def _(sp):
            with sp.Fori(0, HU // 2) as i:
                for s in range(2):
                    g = 2 * i + s
                    sp.wait_ge(S["t_up"], g + 1)
                    waited(sp, S["sync_waited"])
                    for h in range(2):
                        sp.dma_start(vr[s][:, :, h, :], c.src_rows[bass.ds(g * UE + h * HALF, UE), :]
                                     .rearrange("(p k) d -> p k d", k=T)).then_inc(S[f"rows_in{s}"], 16)
                    sp.wait_ge(S["filled"], g + 1)
                    waited(sp, S["sync_waited"])
                    sp.dma_start(fm[s][:, :], spread_marks(c.same, g)).then_inc(S[f"fm_in{s}"], 16)

        @block.gpsimd
        def _(pool):
            with pool.Fori(0, HU // 2) as i:
                for s in range(2):
                    g = 2 * i + s
                    pool.wait_ge(S["staged"], g + 2)
                    pool.wait_ge(S["t_up"], g + 1)
                    waited(pool, S["pool_waited"])
                    for h in range(2):
                        for k in range(T):
                            nc.gpsimd.indirect_dma_start(
                                q[s][:, k, h, :], None, c.node_rows,
                                bass.IndirectOffsetOnAxis(idx[s][:, k, h:h + 1], 0)).then_inc(S[f"gathered{s}"], 16)

        @block.tensor
        def _(pe):
            pe.sem_inc(S["t_up"], 1)
            with pe.Fori(0, HU // 2) as i:
                for s in range(2):
                    pe.wait_ge(S[f"gathered{s}"], 128 * (i + 1))
                    pe.wait_ge(S[f"rows_in{s}"], 32 * (i + 1) + 1)
                    pe.wait_ge(S["added"], 2 * i + s + 1)
                    for rows, up in ((q, qt), (vr, vt)):
                        for k in range(T):
                            mm = nc.tensor.transpose(by_tile(up[s][:, :])[:, k, :],
                                                     rows[s][:, k, :, :].rearrange("p h d -> p (h d)"), c.ident[:, :])
                    mm.then_inc(S["t_up"], 1)

        @block.scalar
        def _(act):
            def stage(g):
                for h in range(2):
                    last = nc.scalar.copy(idx[g.s][:, :, h], c.dsti[:, bass.ds((g.n + h * HU) * T, T)])
                last.then_inc(S["staged"], 1)

            def give(g):
                act.wait_ge(S["added"], g.n + 3)
                act.dma_start(c.u_dram[bass.ds(g.n * P, P), :], u[g.s][:, :]).then_inc(S[f"stored{g.s}"], 16)

            zero = Turn(0, 0)
            stage(zero)
            stage(zero + 1)
            act.wait_ge(S["gathered0"], 128)
            stage(zero + 2)
            give(zero)

            def body(g, more=True):
                if more:
                    act.wait_ge(S[f"gathered{g.s}"], 128 * (g.q + 1))
                    stage(g + 2)
                give(g)

            turns(act, body, 1, LOOPS, HU - 2)
            last = Turn(HU // 2 - 1, 0)
            body(last, more=False)
            body(last + 1, more=False)
            for s in range(2):
                act.wait_ge(S[f"stored{s}"], 16 * (HU // 2) + 1)

        @block.vector
        def _(dve):
            v = nc.vector
            v.memset(stats[:, :], 0.0).then_inc(S["filled"], 1)
            dve.wait_ge(S["filled"], 2)
            v.memset(a[1][:, UE - 1:UE], 0.0).then_inc(S["added"], 1)
            dve.wait_ge(S["added"], 2)

            def body(g, real=(UE, UE)):
                dve.wait_ge(S["t_up"], g.n + 3)
                dve.wait_ge(S[f"fm_in{g.s}"], 16 * (g.q + 1) + 1)
                v.tensor_tensor_scan(a[g.s][:, :], fm[g.s][:, :], vt[g.s][:, :], a[1 - g.s][:, UE - 1:UE], ALU.mult,
                                     ALU.add).then_inc(S["filled"], 1)
                dve.wait_ge(S["filled"], g.n + 3)
                dve.wait_ge(S[f"stored{g.s}"], 16 * g.q + 1)
                v.tensor_tensor(u[g.s][:, :], a[g.s][:, :], qt[g.s][:, :], ALU.add).then_inc(S["added"], 1)
                dve.wait_ge(S["added"], g.n + 3)
                at = stats[:, bass.ds(g.n * 6, 6)]
                if real[0] == real[1]:
                    v.bn_stats(at, u[g.s][:, :])
                else:
                    for h, n in enumerate(real):
                        if n:
                            v.bn_stats(at[64 * h:64 * h + 64, :], u[g.s][64 * h:64 * h + 64, 0:n])

            with dve.Fori(0, HU // 2 - 1) as i:
                body(Turn(i, 0))
                body(Turn(i, 1))
            last = Turn(HU // 2 - 1, 0)
            body(last, (UE, REST))
            body(last + 1, (UE, 0))


def norm_params(c, stats, mean, var):
    nc = c.nc
    n = c.normed
    c.normed += 1
    step, pes = c.norm_sems
    with ExitStack() as local:
        def sb(name, shape):
            return local.enter_context(nc.sbuf_tensor(c.fresh(name), shape, F32))

        fold = sb("fold", [P, P])
        mv, t, share = sb("mv", [P, 2]), sb("np_t", [P, 2]), sb("share", [P, 1])
        ps = local.enter_context(nc.psum_tensor(c.fresh("fold_ps"), [P, 512], F32))
        block = local.enter_context(nc.Block())

        @block.vector
        def _(dve):
            v = nc.vector
            st = Steps(dve, step, 9 * n)
            v.memset(share[0:64, :], HALF / E)
            v.memset(share[64:128, :], (E - HALF) / E)
            v.tensor_tensor(fold[:, 0:64], c.ident[:, 0:64], c.ident[:, 64:128], ALU.add)
            v.bn_aggr(mv[0:64, :], stats[0:64, 0:HU * 6])
            st.run(v.bn_aggr(mv[64:128, :], stats[64:128, 0:(HU - 1) * 6]))
            v.tensor_copy(fold[:, 64:128], fold[:, 0:64])
            st.run(v.tensor_scalar(t[:, :], mv[:, :], share[:, 0:1], None, ALU.mult))
            dve.wait_ge(pes, 2 * n + 1)
            st.run(v.tensor_copy(mean, ps[:, 0:1]))
            st.run(v.tensor_copy(var, ps[:, 1:2]))
            st.run(v.tensor_tensor(mv[:, 0:1], mv[:, 0:1], mean, ALU.subtract))
            st.run(v.tensor_tensor(mv[:, 1:2], mv[:, 0:1], mv[:, 0:1], ALU.mult))
            st.run(v.tensor_scalar(t[:, 0:1], mv[:, 1:2], share[:, 0:1], None, ALU.mult))
            dve.wait_ge(pes, 2 * n + 2)
            st.run(v.tensor_tensor(var, var, ps[:, 2:3], ALU.add))
            st.run(v.tensor_scalar(var, var, BN_EPS, None, ALU.add))
            assert st.n == 9

        @block.tensor
        def _(pe):
            pe.wait_ge(step, 9 * n + 2)
            nc.tensor.matmul(ps[:, 0:2], fold[:, :], t[:, :], start=True, stop=True).then_inc(pes, 1)
            pe.wait_ge(step, 9 * n + 7)
            nc.tensor.matmul(ps[:, 2:3], fold[:, :], t[:, 0:1], start=True, stop=True).then_inc(pes, 1)


def layer2_second(c, stats, gain, shift, w2):
    nc = c.nc
    names = ("sync_waited", "z_made", "y_up", "u_in0", "u_in1", "neg_in0", "neg_in1", "seg_made", "seg_begun",
             "out_up", "out_copied", "stored0", "stored1")
    S = {n: c.sem("l2b_" + n) for n in names}
    start_at_one(c, [sem for name, sem in S.items() if not name.startswith("gathered")])
    with ExitStack() as local:
        def two(name, shape):
            return [local.enter_context(nc.sbuf_tensor(f"l2b_{name}{s}", shape, F32)) for s in range(2)]

        u, z, neg, seg = (two(n, [P, UE]) for n in ("u", "z", "neg", "seg"))
        ob = two("ob", [P, 2, T, D])
        y, ot = ([local.enter_context(nc.psum_tensor(f"l2b_{n}{s}", [P, UE], F32)) for s in range(2)]
                 for n in ("y", "ot"))
        block = local.enter_context(nc.Block())

        @block.sync
        def _(sp):
            with sp.Fori(0, HU // 2) as i:
                for s in range(2):
                    g = 2 * i + s
                    sp.wait_ge(S["z_made"], g + 1)
                    waited(sp, S["sync_waited"])
                    sp.dma_start(u[s][:, :], c.u_dram[bass.ds(g * P, P), :]).then_inc(S[f"u_in{s}"], 16)
                    sp.wait_ge(S["seg_made"], g + 1)
                    waited(sp, S["sync_waited"])
                    sp.dma_start(neg[s][:, :], spread_marks(c.breaks, g)).then_inc(S[f"neg_in{s}"], 16)

        @block.scalar
        def _(act):
            a_ = nc.scalar

            def start(g):
                act.wait_ge(S[f"u_in{g.s}"], 16 * (g.q + 1) + 1)
                act.wait_ge(S["y_up"], g.n + 1)
                a_.activation(z[g.s][:, :], u[g.s][:, :], ACT.Relu, bias=shift, scale=gain).then_inc(S["z_made"], 1)

            def give(g):
                act.wait_ge(S["out_up"], g.n + 2)
                act.wait_ge(S[f"stored{g.s}"], 16 * g.q + 1)
                a_.copy(ob[g.s][:, :, :, :].rearrange("p h k d -> p k h d"),
                        ot[g.s][:, :].rearrange("p (k h d) -> p k h d", k=T, h=2))\
                    .then_inc(S["out_copied"], 1)
                act.wait_ge(S["out_copied"], g.n + 2)
                act.dma_start(group_rows(c.seg_rows, g.n), ob[g.s][:, :, :, :].rearrange("p h k d -> p h (k d)"))\
                   .then_inc(S[f"stored{g.s}"], 16)

            act.sem_inc(S["z_made"], 1)
            zero = Turn(0, 0)
            start(zero)
            start(zero + 1)

            def body(g, more=True):
                if more:
                    start(g + 2)
                give(g)

            with act.Fori(0, HU // 2 - 1) as i:
                body(Turn(i, 0))
                body(Turn(i, 1))
            last = Turn(HU // 2 - 1, 0)
            body(last, more=False)
            body(last + 1, more=False)
            for s in range(2):
                act.wait_ge(S[f"stored{s}"], 16 * (HU // 2) + 1)

        @block.tensor
        def _(pe):
            pe.sem_inc(S["y_up"], 1)

            def product(g):
                pe.wait_ge(S["z_made"], g.n + 3)
                pe.wait_ge(S["seg_made"], g.n + 1)
                nc.tensor.matmul(y[g.s][:, :], w2, z[g.s][:, :], start=True, stop=True).then_inc(S["y_up"], 1)

            def out(g):
                pe.wait_ge(S["seg_made"], g.n + 3)
                pe.wait_ge(S["out_copied"], g.n + 1)
                for k in range(T):
                    mm = nc.tensor.transpose(ot[g.s][:, k * P:(k + 1) * P],
                                             seg[g.s][:, :].rearrange("p (e k) -> p k e", k=T)[:, k, :],
                                             c.ident[:, :])
                mm.then_inc(S["out_up"], 1)

            zero = Turn(0, 0)
            product(zero)

            def body(g, more=True):
                if more:
                    product(g + 1)
                out(g)

            with pe.Fori(0, HU // 2 - 1) as i:
                body(Turn(i, 0))
                body(Turn(i, 1))
            last = Turn(HU // 2 - 1, 0)
            body(last)
            body(last + 1, more=False)

        @block.vector
        def _(dve):
            v = nc.vector
            v.memset(stats[:, :], 0.0)
            v.memset(seg[1][:, UE - 1:UE], -BIG).then_inc(S["seg_begun"], 1)
            dve.wait_ge(S["seg_begun"], 2)
            dve.sem_inc(S["seg_made"], 1)

            def body(g, real=(UE, UE)):
                dve.wait_ge(S["y_up"], g.n + 3)
                at = stats[:, bass.ds(g.n * 6, 6)]
                if real[0] == real[1]:
                    v.bn_stats(at, y[g.s][:, :])
                else:
                    for h, n in enumerate(real):
                        if n:
                            v.bn_stats(at[64 * h:64 * h + 64, :], y[g.s][64 * h:64 * h + 64, 0:n])
                dve.wait_ge(S[f"neg_in{g.s}"], 16 * (g.q + 1) + 1)
                dve.wait_ge(S["seg_made"], g.n + 2)
                v.tensor_tensor_scan(seg[g.s][:, :], neg[g.s][:, :], y[g.s][:, :], seg[1 - g.s][:, UE - 1:UE],
                                     ALU.add, ALU.max).then_inc(S["seg_made"], 1)

            with dve.Fori(0, HU // 2 - 1) as i:
                body(Turn(i, 0))
                body(Turn(i, 1))
            last = Turn(HU // 2 - 1, 0)
            body(last, (UE, REST))
            body(last + 1, (UE, 0))


def mark_breaks(c):
    nc = c.nc
    moved, made = c.sem("breaks_moved"), c.sem("breaks_made")
    with ExitStack() as local:
        marks = local.enter_context(nc.sbuf_tensor("all_marks", [P, EP // P], F32))
        block = local.enter_context(nc.Block())

        @block.sync
        def _(sp):
            sp.dma_start(marks[:, :], c.same[0:EP, :].rearrange("(p r) o -> p (r o)", p=P)).then_inc(moved, 16)
            sp.wait_ge(made, 1)
            sp.dma_start(c.breaks.rearrange("(p r) o -> p (r o)", p=P), marks[:, :]).then_inc(moved, 16)
            sp.wait_ge(moved, 32)

        @block.vector
        def _(dve):
            dve.wait_ge(moved, 16)
            nc.vector.tensor_scalar(marks[:, :], marks[:, :], 1.0, BIG, ALU.subtract, ALU.mult).then_inc(made, 1)


def layer2(c, w1, b1, g1, be1, w2, b2, g2, be2):
    nc = c.nc
    with ExitStack() as local:
        def sb(name, shape, dt=F32):
            return local.enter_context(nc.sbuf_tensor("l2n_" + name, shape, dt))

        h, pq = sb("h", [P, NJ, D]), sb("pq", [P, NJ, 2 * D])
        wp, bp = sb("wp", [D, 2 * D]), sb("bp", [P, 2 * D])
        w2s, sgn = sb("w2", [P, P]), sb("sgn", [P, P])
        cols = sb("cols", [P, 2])
        rows = sb("rows", [P, 3, D])
        mean, var, root = sb("mean", [P, 1]), sb("var", [P, 1]), sb("root", [P, 1])
        gain, shift = sb("gain", [P, 1]), sb("shift", [P, 1])
        stats = sb("stats", [P, HU * 6])
        step, acts = c.sem("l2n_step"), c.sem("l2n_act")
        normalise(c, h[:, :, :], c.ln_sems, 2)
        with nc.Block() as block:
            @block.vector
            def _(dve):
                nc.vector.memset(bp[:, :], 0.0)
                nc.vector.memset(w2s[:, :], 0.0)
        load_all(c, [(wp[:, 0:D], w1[0:D, :]), (wp[:, D:2 * D], w1[D:2 * D, :]),
                     (bp[:, 0:D], b1.partition_broadcast(P)), (w2s[0:D, 0:D], w2), (w2s[D:2 * D, D:2 * D], w2),
                     (sgn[:, 0:D], g2.partition_broadcast(P)), (sgn[:, D:2 * D], g2.partition_broadcast(P)),
                     (rows[:, 0, :], g2.partition_broadcast(P)), (rows[:, 1, :], be2.partition_broadcast(P)),
                     (rows[:, 2, :], b2.partition_broadcast(P))]
                 + [(cols[D * k:D * k + D, n:n + 1], column(x)) for n, x in enumerate((g1, be1)) for k in range(2)])
        with nc.Block() as block:
            @block.vector
            def _(dve):
                v = nc.vector
                st = Steps(dve, step)
                v.tensor_tensor(wp[:, 0:D], wp[:, 0:D], wp[:, D:2 * D], ALU.subtract)
                st.run(v.tensor_scalar(sgn[:, :], sgn[:, :], 0.0, None, ALU.is_ge))
                st.run(v.tensor_scalar(sgn[:, :], sgn[:, :], 2.0, -1.0, ALU.mult, ALU.add))
                v.tensor_tensor(w2s[:, :], w2s[:, :], sgn[:, :], ALU.mult)
                st.run(v.tensor_tensor(rows[:, 2, :], rows[:, 2, :], sgn[:, 0:D], ALU.mult))
        project(c, h, wp[:, :], bp[:, :], pq, 2 * D)
        place_rows(c, pq[:, :, 0:D], D, c.node_rows, c.src_rows, table_rows=pq[:, :, D:2 * D])
        mark_breaks(c)
        layer2_first(c, stats)
        norm_params(c, stats, mean[:, :], var[:, :])
        with nc.Block() as block:
            @block.scalar
            def _(act):
                nc.scalar.activation(root[:, :], var[:, :], ACT.Sqrt).then_inc(acts, 1)

            @block.vector
            def _(dve):
                v = nc.vector
                st = Steps(dve, step, 3)
                dve.wait_ge(acts, 1)
                st.run(v.reciprocal(root[:, :], root[:, :]))
                st.run(v.tensor_tensor(gain[:, :], root[:, :], cols[:, 0:1], ALU.mult))
                st.run(v.tensor_tensor(shift[:, :], mean[:, :], gain[:, :], ALU.mult))
                st.run(v.tensor_tensor(shift[:, :], cols[:, 1:2], shift[:, :], ALU.subtract))
        layer2_second(c, stats, gain[:, 0:1], shift[:, 0:1], w2s[:, :])
        norm_params(c, stats, mean[:, :], var[:, :])
        agg, carry = h, sb("carry", [P, D])
        fetch_ends(c, c.seg_rows, D, agg, carry[:, :])
        tt = sb("tt", [P, NJ, D])
        mrow, vrow = sb("mrow", [P, D]), sb("vrow", [P, D])
        crow, lim = sb("crow", [P, NJ]), sb("lim", [P, NJ])
        moved = c.sem("l2n_moved")
        with nc.Block() as block:
            @block.sync
            def _(sp):
                sp.dma_start(column(c.mean_dram), mean[0:D, :]).then_inc(moved, 16)
                sp.dma_start(column(c.var_dram), var[0:D, :]).then_inc(moved, 16)
                sp.wait_ge(moved, 32)
                sp.dma_start(mrow[:, :], c.mean_dram.partition_broadcast(P)).then_inc(moved, 16)
                sp.dma_start(vrow[:, :], c.var_dram.partition_broadcast(P)).then_inc(moved, 16)

            @block.scalar
            def _(act):
                act.wait_ge(moved, 64)
                nc.scalar.activation(vrow[:, :], vrow[:, :], ACT.Sqrt).then_inc(acts, 1)

            @block.vector
            def _(dve):
                v = nc.vector
                st = Steps(dve, step, 7)
                dve.wait_ge(acts, 2)
                st.run(v.reciprocal(vrow[:, :], vrow[:, :]))
                st.run(v.tensor_tensor(rows[:, 0, :], rows[:, 0, :], sgn[:, 0:D], ALU.mult))
                st.run(v.tensor_tensor(vrow[:, :], vrow[:, :], rows[:, 0, :], ALU.mult))
                st.run(v.tensor_tensor(mrow[:, :], mrow[:, :], rows[:, 2, :], ALU.add))
                st.run(v.tensor_tensor(mrow[:, :], mrow[:, :], vrow[:, :], ALU.mult))
                st.run(v.tensor_tensor(mrow[:, :], rows[:, 1, :], mrow[:, :], ALU.subtract))
                st.run(v.tensor_scalar(crow[:, :], c.cross[:, :], BIG, -BIG, ALU.mult, ALU.add))
                st.run(v.tensor_tensor(tt[:, :, :], spread(c.cross[:, :], D), spread_mid(carry[:, :], NJ), ALU.mult))
                st.run(v.tensor_tensor(tt[:, :, :], tt[:, :, :], spread(crow[:, :], D), ALU.add))
                st.run(v.tensor_tensor(agg[:, :, :], agg[:, :, :], tt[:, :, :], ALU.max))
                st.run(v.tensor_tensor(agg[:, :, :], agg[:, :, :], spread_mid(rows[:, 2, :], NJ), ALU.add))
                st.run(v.tensor_tensor(agg[:, :, :], agg[:, :, :], spread_mid(vrow[:, :], NJ), ALU.mult))
                st.run(v.tensor_tensor(agg[:, :, :], agg[:, :, :], spread_mid(mrow[:, :], NJ), ALU.add))
                st.run(v.tensor_scalar(lim[:, :], c.keep[:, :], 1.0, 3e38, ALU.subtract, ALU.mult))
                st.run(v.tensor_scalar(lim[:, :], lim[:, :], 10.0, None, ALU.mult))
                st.run(v.scalar_tensor_tensor(agg[:, :, :], agg[:, :, :], 0.0, spread(lim[:, :], D), ALU.max,
                                              ALU.add))
                st.run(v.tensor_tensor(c.xs[:, :, :], c.xs[:, :, :], agg[:, :, :], ALU.add))


def layer3_edges(c, w_attr, w2, b2):
    nc = c.nc
    DF = DE + 1
    names = ("pool_waited", "sync_waited", "staged",
             "t_up", "feat_up", "feat_kept", "pre_up", "filled", "summed", "hid_made", "msg_up", "msg_made",
             "seg_made", "out_up", "out_copied", "gathered0", "gathered1", "rows_in0", "rows_in1", "feat_in0",
             "feat_in1", "fm_in0", "fm_in1", "sm_in0", "sm_in1", "stored0", "stored1", "part_made")
    S = {n: c.sem("l3_" + n) for n in names}
    start_at_one(c, [sem for name, sem in S.items() if not name.startswith("gathered")])
    LOOPS = (UNITS - 6) // 2
    with ExitStack() as local:
        def sb(name, shape, dt=F32):
            return local.enter_context(nc.sbuf_tensor("l3_" + name, shape, dt))

        def two(name, shape, dt=F32):
            return [sb(f"{name}{s}", shape, dt) for s in range(2)]

        idx = two("idx", [P, T], I32)
        q, vr, ob = (two(n, [P, T, HID]) for n in ("q", "vr", "ob"))
        rec = two("rec", [P, T, RW])
        feat = two("feat", [DF, UE])
        fm, sm, a, part, total, hid, msg, seg = (two(n, [P, UE]) for n in
                                                 ("fm", "sm", "a", "part", "total", "hid", "msg", "seg"))
        ft, pre, my, ot = (local.enter_context(nc.psum_tensor("l3_p" + n, [P, UE], F32)) for n in
                           ("ft", "pre", "my", "ot"))
        qt, vt = ([local.enter_context(nc.psum_tensor(f"l3_{n}{s}", [P, UE], F32)) for s in range(2)]
                  for n in ("qt", "vt"))
        block = local.enter_context(nc.Block())

        def by_tile(ap):
            return ap.rearrange("p (e k) -> p k e", k=T)

        @block.sync
        def _(sp):
            def marks(buf, g, sem):
                sp.dma_start(buf[g.s][:, :], c.same[bass.ds(g.n * UE, UE), :].rearrange("e o -> (e o)")
                             .partition_broadcast(P)).then_inc(S[f"{sem}{g.s}"], 16)

            def rows_and_marks(g):
                if used(g.q):
                    sp.wait_ge(S["t_up"], g.n + 1)
                    waited(sp, S["sync_waited"])
                sp.dma_start(rec[g.s][:, :, :], c.records[bass.ds(g.n * UE, UE), :]
                             .rearrange("(p k) d -> p k d", k=T)).then_inc(S[f"feat_in{g.s}"], 16)
                sp.dma_start(vr[g.s][:, :, :], c.src_wide[bass.ds(g.n * UE, UE), :]
                             .rearrange("(p k) d -> p k d", k=T)).then_inc(S[f"rows_in{g.s}"], 16)
                if used(g.q):
                    sp.wait_ge(S["filled"], g.n + 1)
                    waited(sp, S["sync_waited"])
                marks(fm, g, "fm_in")

            def body(g):
                rows_and_marks(g)
                if used((g - 1).q):
                    sp.wait_ge(S["seg_made"], g.n)
                    waited(sp, S["sync_waited"])
                marks(sm, g - 1, "sm_in")

            zero = Turn(0, 0)
            rows_and_marks(zero)
            body(zero + 1)
            body(zero + 2)
            turns(sp, body, 3, LOOPS - 1, UNITS)
            sp.wait_ge(S["seg_made"], UNITS)
            marks(sm, Turn(UNITS // 2 - 1, 1), "sm_in")

        @block.gpsimd
        def _(pool):
            with pool.Fori(0, UNITS // 2) as i:
                for s in range(2):
                    pool.wait_ge(S["staged"], 2 * i + s + 2)
                    pool.wait_ge(S["t_up"], 2 * i + s + 1)
                    waited(pool, S["pool_waited"])
                    for k in range(T):
                        nc.gpsimd.indirect_dma_start(
                            q[s][:, k, :], None, c.node_wide,
                            bass.IndirectOffsetOnAxis(idx[s][:, k:k + 1], 0)).then_inc(S[f"gathered{s}"], 16)

        @block.tensor
        def _(pe):
            t = nc.tensor
            pe.sem_inc(S["t_up"], 1)

            def feature_turn(g):
                pe.wait_ge(S[f"feat_in{g.s}"], 16 * (g.q + 1) + 1)
                pe.wait_ge(S["feat_kept"], g.n + 1)
                for k in range(T):
                    mm = t.transpose(by_tile(ft[0:DF, :])[:, k, :], rec[g.s][:, k, 0:DF], c.ident[:, :])
                mm.then_inc(S["feat_up"], 1)

            def turn(g):
                pe.wait_ge(S[f"gathered{g.s}"], 64 * (g.q + 1))
                pe.wait_ge(S[f"rows_in{g.s}"], 16 * (g.q + 1) + 1)
                if used(g.q):
                    pe.wait_ge(S["part_made"], g.n)
                for rows, up in ((q, qt), (vr, vt)):
                    for k in range(T):
                        mm = t.transpose(by_tile(up[g.s][:, :])[:, k, :], rows[g.s][:, k, :], c.ident[:, :])
                mm.then_inc(S["t_up"], 1)

            def features(g):
                pe.wait_ge(S["feat_kept"], g.n + 2)
                pe.wait_ge(S["summed"], g.n + 1)
                t.matmul(pre[:, :], w_attr, feat[g.s][:, :], start=True, stop=True).then_inc(S["pre_up"], 1)

            def second(g):
                pe.wait_ge(S["hid_made"], g.n + 2)
                pe.wait_ge(S["msg_made"], g.n + 1)
                t.matmul(my[:, :], w2, hid[g.s][:, :], start=True, stop=True).then_inc(S["msg_up"], 1)

            def out(g):
                pe.wait_ge(S["seg_made"], g.n + 3)
                pe.wait_ge(S["out_copied"], g.n + 1)
                for k in range(T):
                    mm = t.transpose(ot[:, k * P:(k + 1) * P], by_tile(seg[g.s][:, :])[:, k, :], c.ident[:, :])
                mm.then_inc(S["out_up"], 1)

            zero = Turn(0, 0)
            feature_turn(zero)
            turn(zero)
            features(zero)
            feature_turn(zero + 1)
            turn(zero + 1)

            def body(g, ahead=(1, 2), back=True):
                if 2 in ahead:
                    feature_turn(g + 2)
                if 1 in ahead:
                    features(g + 1)
                second(g)
                if back:
                    out(g - 1)
                if 2 in ahead:
                    turn(g + 2)

            body(zero, back=False)
            turns(pe, body, 1, LOOPS, UNITS - 2)
            last = Turn(UNITS // 2 - 1, 1)
            body(last - 1, ahead=(1,))
            body(last, ahead=())
            out(last)

        @block.scalar
        def _(act):
            a_ = nc.scalar

            def stage(g):
                a_.copy(idx[g.s][:, :], c.dsti[:, bass.ds(g.n * T, T)]).then_inc(S["staged"], 1)

            def first(g):
                act.wait_ge(S["feat_up"], g.n + 2)
                a_.copy(feat[g.s][:, :], ft[0:DF, :]).then_inc(S["feat_kept"], 1)

            def hidden(g):
                act.wait_ge(S["summed"], g.n + 2)
                a_.activation(hid[g.s][:, :], total[g.s][:, :], ACT.Silu).then_inc(S["hid_made"], 1)

            def message(g):
                act.wait_ge(S["msg_up"], g.n + 2)
                act.wait_ge(S["seg_made"], g.n + 1)
                a_.activation(msg[g.s][:, :], my[:, :], ACT.Silu, bias=b2).then_inc(S["msg_made"], 1)

            def give(g):
                act.wait_ge(S["out_up"], g.n + 2)
                act.wait_ge(S[f"stored{g.s}"], 16 * g.q + 1)
                a_.copy(ob[g.s][:, :, :], ot[:, :].rearrange("p (k d) -> p k d", k=T)).then_inc(S["out_copied"], 1)
                act.wait_ge(S["out_copied"], g.n + 2)
                act.dma_start(c.seg_wide[bass.ds(g.n * UE, UE), :].rearrange("(p k) d -> p k d", k=T),
                              ob[g.s][:, :, :]).then_inc(S[f"stored{g.s}"], 16)

            zero = Turn(0, 0)
            stage(zero)
            stage(zero + 1)
            first(zero)
            first(zero + 1)
            for g in range(2):
                act.wait_ge(S[f"gathered{g}"], 64)
                stage(zero + 2 + g)
            hidden(zero)

            def body(g, ahead=(1, 2, 4), back=True):
                if 2 in ahead:
                    first(g + 2)
                message(g)
                if 1 in ahead:
                    hidden(g + 1)
                if back:
                    give(g - 1)
                if 4 in ahead:
                    h = g + 2
                    act.wait_ge(S[f"gathered{h.s}"], 64 * (h.q + 1))
                    stage(g + 4)

            body(zero, back=False)
            turns(act, body, 1, LOOPS, UNITS - 4)
            last = Turn(UNITS // 2 - 1, 1)
            body(last - 3, ahead=(1, 2))
            body(last - 2, ahead=(1, 2))
            body(last - 1, ahead=(1,))
            body(last, ahead=())
            give(last)
            for s in range(2):
                act.wait_ge(S[f"stored{s}"], 16 * (UNITS // 2) + 1)

        @block.vector
        def _(dve):
            v = nc.vector
            v.memset(a[1][:, UE - 1:UE], 0.0).then_inc(S["filled"], 1)
            v.memset(seg[1][:, UE - 1:UE], 0.0).then_inc(S["seg_made"], 1)
            dve.wait_ge(S["seg_made"], 2)

            def fill(g):
                dve.wait_ge(S["t_up"], g.n + 3)
                dve.wait_ge(S[f"fm_in{g.s}"], 16 * (g.q + 1) + 1)
                dve.wait_ge(S["filled"], g.n + 2)
                v.tensor_tensor_scan(a[g.s][:, :], fm[g.s][:, :], vt[g.s][:, :], a[1 - g.s][:, UE - 1:UE], ALU.mult,
                                     ALU.add).then_inc(S["filled"], 1)
                dve.wait_ge(S["filled"], g.n + 3)
                v.tensor_tensor(part[g.s][:, :], a[g.s][:, :], qt[g.s][:, :], ALU.add).then_inc(S["part_made"], 1)
                dve.wait_ge(S["part_made"], g.n + 2)
                dve.wait_ge(S["pre_up"], g.n + 2)
                v.tensor_tensor(total[g.s][:, :], part[g.s][:, :], pre[:, :], ALU.add).then_inc(S["summed"], 1)

            def gather_up(g):
                dve.wait_ge(S["msg_made"], g.n + 2)
                dve.wait_ge(S["seg_made"], g.n + 2)
                dve.wait_ge(S[f"sm_in{g.s}"], 16 * (g.q + 1) + 1)
                v.tensor_tensor_scan(seg[g.s][:, :], sm[g.s][:, :], msg[g.s][:, :], seg[1 - g.s][:, UE - 1:UE],
                                     ALU.mult, ALU.add).then_inc(S["seg_made"], 1)

            zero = Turn(0, 0)
            fill(zero)
            fill(zero + 1)
            gather_up(zero)

            def body(g, more=True):
                if more:
                    fill(g + 1)
                gather_up(g)

            turns(dve, body, 1, LOOPS, UNITS - 1)
            body(Turn(UNITS // 2 - 1, 1), more=False)


def layer3(c, ew1, eb1, ew2, eb2, nw1, nb1, nw2, nb2):
    nc = c.nc
    with ExitStack() as local:
        def sb(name, shape, dt=F32):
            return local.enter_context(nc.sbuf_tensor("l3n_" + name, shape, dt))

        h = sb("h", [P, NJ, D])
        w_src, w_dst, w_attr, w_hid = sb("w_src", [D, HID]), sb("w_dst", [D, HID]), sb("w_attr", [DE + 1, HID]), \
            sb("w_hid", [HID, HID])
        b_src, b_no, b_hid = sb("b_src", [P, HID]), sb("b_no", [P, HID]), sb("b_hid", [HID, 1])
        nw_x, nw_a, nw_o = sb("nw_x", [D, HID]), sb("nw_a", [HID, HID]), sb("nw_o", [HID, D])
        nb_h, nb_o = sb("nb_h", [HID, 1]), sb("nb_o", [P, D])
        agg = sb("agg", [P, NJ, HID])
        step = c.sem("l3n_step")
        normalise(c, h[:, :, :], c.ln_sems, 3)
        load_all(c, [(w_src[:, :], ew1[0:D, :]), (w_dst[:, :], ew1[D:2 * D, :]),
                     (w_attr[:, :], ew1[2 * D:2 * D + DE + 1, :]), (w_hid[:, :], ew2),
                     (b_src[:, :], eb1.partition_broadcast(P)), (b_hid[:, :], column(eb2)),
                     (nw_x[:, :], nw1[0:D, :]), (nw_a[:, :], nw1[D:D + HID, :]), (nw_o[:, :], nw2),
                     (nb_h[:, :], column(nb1)), (nb_o[:, :], nb2.partition_broadcast(P))])
        with nc.Block() as block:
            @block.vector
            def _(dve):
                nc.vector.memset(b_no[:, :], 0.0)
        with ExitStack() as wide:
            rows = wide.enter_context(nc.sbuf_tensor("l3n_rows", [P, NJ, HID], F32))
            project(c, h, w_src[:, :], b_src[:, :], rows, HID)
            place_rows(c, rows[:, :, :], HID, None, c.src_wide)
            project(c, h, w_dst[:, :], b_no[:, :], rows, HID)
            with nc.Block() as block:
                @block.sync
                def _(sp):
                    sp.dma_start(c.node_wide.rearrange("(p j) d -> p j d", p=P), rows[:, :, :]).then_inc(step, 16)
                    sp.wait_ge(step, 16)
        layer3_edges(c, w_attr[:, :], w_hid[:, :], b_hid[:, 0:1])
        fetch_ends(c, c.seg_wide, HID, agg, None)
        with nc.Block() as block:
            @block.vector
            def _(dve):
                nc.vector.tensor_tensor(agg[:, :, :], agg[:, :, :], spread(c.has[:, :], HID), ALU.mult)
        perceptron(c, [(h, D, nw_x[:, :]), (agg, HID, nw_a[:, :])], nb_h[:, :], ACT.Silu, [], nw_o[:, :], nb_o[:, :],
                   h)


def store_x(c, out):
    nc = c.nc
    full = N // NJ
    with nc.Block() as block:
        @block.sync
        def _(sp):
            sp.dma_start(out[0:full * NJ, :].rearrange("(p j) d -> p j d", p=full), c.xs[0:full]).then_inc(c.out_sem, 16)
            sp.dma_start(out[full * NJ:N, :].rearrange("(p j) d -> p j d", p=1),
                         c.xs[full:full + 1, 0:N - full * NJ, :]).then_inc(c.out_sem, 16)
            sp.wait_ge(c.out_sem, 32)


def fresh(c, name):
    c.names += 1
    return f"{name}{c.names}"


def gnn(nc, ins, out):
    with ExitStack() as whole:
        c = Core()
        c.nc = nc
        c.sem = lambda name: whole.enter_context(nc.semaphore(name))
        (c.x, c.src, c.dst, c.edge_attr_16, c.edge_attr_64, c.edge_weight, c.edge_weight_n2) = ins[:7]
        c.deg_coeff = ins[9]

        def scratch(name, shape):
            return nc.dram_tensor(name, shape, F32, kind="Internal").ap()

        c.agg_parts = [scratch(f"agg_part{t}", [NP + P, D + 1]) for t in range(TABLES)]
        c.src_rows = scratch("src_rows", [EP + NP, D])
        c.src_wide = scratch("src_wide", [EP + NP, HID])
        c.same = scratch("same_as_before", [EP + NP, 1])
        c.breaks = scratch("breaks", [EP, 1])
        c.records = scratch("records", [EP, RW])
        c.start_dram = scratch("start_dram", [NP])
        c.count_dram = scratch("count_dram", [NP])
        c.normed_rows = [scratch(f"normed_rows{h}", [NP, D + 1]) for h in range(2)]
        c.node_rows = scratch("node_rows", [NP, D])
        c.node_wide = scratch("node_wide", [NP, HID])
        c.seg_rows = scratch("seg_rows", [EP, D])
        c.seg_wide = scratch("seg_wide", [EP, HID])
        c.u_dram = scratch("u_dram", [HU * P, UE])
        c.mean_dram, c.var_dram = scratch("mean_dram", [D]), scratch("var_dram", [D])
        c.names = 0
        c.normed = 0
        c.norm_sems = [c.sem("norm_step"), c.sem("norm_pe")]
        c.more_sem = c.sem("residual_added")
        c.fresh = lambda name: fresh(c, name)
        c.projected = c.loads = c.placed = c.spotted = c.middles = c.fetched = c.carried = 0
        c.project_sems = [c.sem("pj_" + n) for n in ("turned", "taken", "made", "kept")]
        c.load_sem, c.place_sem, c.spot_sem, c.middle_sem, c.fetch_sem, c.carry_sem = (
            c.sem(n) for n in ("weights_in", "rows_placed", "rows_spread", "middle_row", "ends_in", "carry_in"))
        c.out_sem = c.sem("x_out")
        c.ln_sems = [c.sem("ln_step"), c.sem("ln_rooted")]
        c.dsti = whole.enter_context(nc.sbuf_tensor("dsti", [P, (UNITS + 2) * T], I32))
        make_constants(c, whole)
        with ExitStack() as edges:
            KF = edges.enter_context(nc.sbuf_tensor("KF", [P, UNITS * 16], F32))
            KB = edges.enter_context(nc.sbuf_tensor("KB", [P, UNITS * 16], BF16))
            start = edges.enter_context(nc.sbuf_tensor("start", [HI, LO], F32))
            with own_semaphores(c):
                lay_edges(c, KF, KB)
                count_edges(c, KB, start)
            with own_semaphores(c):
                sort_and_aggregate(c, KF, KB, start)
        with own_semaphores(c):
            layer0(c, ins[7], ins[8], ins[10], ins[11])
        with own_semaphores(c):
            layer1(c, *ins[12:18])
        with own_semaphores(c):
            layer2(c, *ins[18:26])
        with own_semaphores(c):
            layer3(c, *ins[26:34])
        store_x(c, out)


_INS = ['x', 'src', 'dst', 'edge_attr_16', 'edge_attr_64', 'edge_weight', 'edge_weight_n2', 'L0_gnn_W', 'L0_gnn_b',
        'L0_gnn_deg_coeff', 'L0_gnn_coeff_param', 'L0_gnn_scale_param', 'L1_gnn_W0', 'L1_gnn_b0', 'L1_gnn_W1',
        'L1_gnn_b1', 'L1_gnn_W2', 'L1_gnn_b2', 'L2_gnn_W1', 'L2_gnn_b1', 'L2_gnn_g1', 'L2_gnn_be1', 'L2_gnn_W2',
        'L2_gnn_b2', 'L2_gnn_g2', 'L2_gnn_be2', 'L3_gnn_ew1', 'L3_gnn_eb1', 'L3_gnn_ew2', 'L3_gnn_eb2', 'L3_gnn_nw1',
        'L3_gnn_nb1', 'L3_gnn_nw2', 'L3_gnn_nb2']


def kernel(**inputs):
    import numpy as _np
    import concourse.bacc as _bacc
    from concourse import mybir as _mybir
    from concourse.bass_utils import run_bass_kernel_spmd as _run

    nc = _bacc.Bacc("TRN2", target_bir_lowering=False, num_devices=1)
    arrays, args = {}, []
    for name in _INS:
        a = _np.ascontiguousarray(inputs[name])
        arrays[f"in_{name}_dram"] = a
        args.append(nc.dram_tensor(f"in_{name}_dram", a.shape, _mybir.dt.from_np(a.dtype), kind="ExternalInput").ap())
    out = nc.dram_tensor("out_0_dram", (N, D), F32, kind="ExternalOutput").ap()
    gnn(nc, args, out)
    r = _run(nc, [arrays], core_ids=[0])
    return r.results[0]["out_0_dram"]
```
